# Optimizing a Trainium2 kernel written in Bass

```python
import numpy as np
import jax
import jax.numpy as jnp

def _softmax(x, axis=-1):
    return jax.nn.softmax(x, axis=axis)

def _gelu(x):
    return jax.nn.gelu(x, approximate=True)

def _silu(x):
    return jax.nn.silu(x)

def _sigmoid(x):
    return jax.nn.sigmoid(x)

def _layernorm(x, axis=-1, eps=1e-05):
    m = jnp.mean(x, axis=axis, keepdims=True)
    v = jnp.var(x, axis=axis, keepdims=True)
    return (x - m) / jnp.sqrt(v + eps)

def _scatter_add(tgt, idx, src, axis=0):
    return tgt.at[idx].add(src)

def _segment_sum(src, seg, n):
    return jax.ops.segment_sum(src, seg, n)
kernel_name = 'mk_flamingo_gated_d2_seqx_r8_35405e'

def setup_inputs(seed: int=0):
    np.random.seed(seed)
    _w = jnp.asarray

    def _rec_inputs():
        import jax
        import jax.numpy as jnp
        _rk = jax.random.key(seed)
        x = -7.109e-05 + 0.9999 * jax.random.normal(jax.random.fold_in(_rk, 1), (4, 256, 256), jnp.float32)
        _lenS = 256 - jax.random.randint(jax.random.fold_in(_rk, 7), (4,), 0, max(1, 256 // 4) + 1, jnp.int32)
        _lenS2 = 256 - jax.random.randint(jax.random.fold_in(_rk, 8), (4,), 0, max(1, 256 // 4) + 1, jnp.int32)
        _ctx_512P = jax.random.normal(jax.random.fold_in(_rk, 11), (4, 16, 64), jnp.float32)
        _ctx_512c = jax.random.dirichlet(jax.random.fold_in(_rk, 511), 0.3 * jnp.ones((16,), jnp.float32), (4, 256))
        _ctx_512t = jnp.einsum('bsk,bkd->bsd', _ctx_512c, _ctx_512P)
        _ctx_512t = _ctx_512t * jax.lax.rsqrt(jnp.mean(jnp.square(_ctx_512t)) + 1e-12) * 0.953939
        ctx_512 = 2.81802e-05 + 1.00001 * (_ctx_512t + 0.3 * jax.random.normal(jax.random.fold_in(_rk, 611), (4, 256, 64), jnp.float32))
        _g = jax.random.normal(jax.random.fold_in(_rk, 9001), (2, 2), jnp.float32)
        _g = jnp.sign(_g) * jnp.maximum(jnp.abs(_g), 1.0) + (_g == 0) * 1.0
        g_xattn = _g[0]
        g_ffn = _g[1]
        return (x, ctx_512, g_xattn, g_ffn)
    x, ctx_512, g_xattn, g_ffn = _rec_inputs()

    def _L0_xattn_setup():
        import jax, jax.numpy as jnp
        import numpy as np
        EPS = 1e-06
        IMAGE_DIMS = 256
        key = jax.random.key(seed)
        k1, k2, k3 = jax.random.split(key, 3)
        B, I, J, D = (16, 256, 256, 64)
        p = jax.random.normal(k1, (B, I, J), dtype=jnp.float32)
        k_v = jax.random.normal(k2, (B, J, D), dtype=jnp.float32)
        W_k = jax.random.normal(k3, (D, D), dtype=jnp.float32) * (1.0 / np.sqrt(D))
        b_k = jnp.zeros((D,), dtype=jnp.float32)
        ln_gamma = jnp.ones((J,), dtype=jnp.float32)
        ln_beta = jnp.zeros((J,), dtype=jnp.float32)
        return {'p': p, 'k_v': k_v, 'W_k': W_k, 'b_k': b_k, 'ln_gamma': ln_gamma, 'ln_beta': ln_beta}
    _L0_xattn_all = _L0_xattn_setup()
    _L0_xattn_in = {k: v for k, v in _L0_xattn_all.items() if k in ('W_k', 'b_k', 'ln_gamma', 'ln_beta')}
    del _L0_xattn_all

    def _L0_ffn_setup():
        import jax, jax.numpy as jnp
        import numpy as np
        B, S, H, F, E, K = (2, 128, 256, 688, 8, 2)
        key = jax.random.key(seed)
        k0, k1, k2, k3, k4 = jax.random.split(key, 5)
        x = jax.random.normal(k0, (B, S, H), dtype=jnp.float32)
        router_w = jax.random.normal(k1, (E, H), dtype=jnp.float32) * 0.02
        gate_w = jax.random.normal(k2, (E, F, H), dtype=jnp.float32) * 0.02
        up_w = jax.random.normal(k3, (E, F, H), dtype=jnp.float32) * 0.02
        down_w = jax.random.normal(k4, (E, H, F), dtype=jnp.float32) * 0.02
        return {'x': x, 'router_w': router_w, 'gate_w': gate_w, 'up_w': up_w, 'down_w': down_w}
    _L0_ffn_all = _L0_ffn_setup()
    _L0_ffn_in = {k: v for k, v in _L0_ffn_all.items() if k in ('router_w', 'gate_w', 'up_w', 'down_w')}
    del _L0_ffn_all

    def _L1_xattn_setup():
        import jax, jax.numpy as jnp
        import numpy as np
        P_ASEM = 0.6
        key = jax.random.key(seed)
        k1, k2, k3 = jax.random.split(key, 3)
        B, N, D = (8, 256, 64)
        x = jax.random.normal(k1, (B, N, D), dtype=jnp.float32)
        adj = jax.random.uniform(k2, (B, N, N), dtype=jnp.float32)
        bound = 1.0 / np.sqrt(2 * D)
        W = jax.random.uniform(k3, (1, 2 * D), dtype=jnp.float32, minval=-bound, maxval=bound)
        b = jnp.zeros((1,), dtype=jnp.float32)
        return {'x': x, 'adj': adj, 'W': W, 'b': b}
    _L1_xattn_all = _L1_xattn_setup()
    _L1_xattn_in = {k: v for k, v in _L1_xattn_all.items() if k in ('W', 'b')}
    del _L1_xattn_all

    def _L1_ffn_setup():
        import jax, jax.numpy as jnp
        import numpy as np
        DIM = 256
        INTER = 176
        N_ROUTED = 15
        TOPK = 2
        SHARED_INTER = 176

        def _swiglu(x, wa, wb, wo):
            return jax.nn.silu(x @ wa.T) * (x @ wb.T) @ wo.T
        key = jax.random.key(seed)
        ks = jax.random.split(key, 8)
        s = 0.02
        return {'x': jax.random.normal(ks[0], (2, 256, DIM), dtype=jnp.float32), 'gate_w': jax.random.normal(ks[1], (N_ROUTED, DIM), dtype=jnp.float32) * s, 'w1': jax.random.normal(ks[2], (N_ROUTED, INTER, DIM), dtype=jnp.float32) * s, 'w3': jax.random.normal(ks[3], (N_ROUTED, INTER, DIM), dtype=jnp.float32) * s, 'w2': jax.random.normal(ks[4], (N_ROUTED, DIM, INTER), dtype=jnp.float32) * s, 'sw1': jax.random.normal(ks[5], (SHARED_INTER, DIM), dtype=jnp.float32) * s, 'sw3': jax.random.normal(ks[6], (SHARED_INTER, DIM), dtype=jnp.float32) * s, 'sw2': jax.random.normal(ks[7], (DIM, SHARED_INTER), dtype=jnp.float32) * s}
    _L1_ffn_all = _L1_ffn_setup()
    _L1_ffn_in = {k: v for k, v in _L1_ffn_all.items() if k in ('gate_w', 'w1', 'w2', 'w3', 'sw1', 'sw2', 'sw3')}
    del _L1_ffn_all
    return {'x': x, 'ctx_512': ctx_512, 'g_xattn': g_xattn, 'g_ffn': g_ffn, 'L0_xattn_W_k': _L0_xattn_in['W_k'], 'L0_xattn_b_k': _L0_xattn_in['b_k'], 'L0_xattn_ln_gamma': _L0_xattn_in['ln_gamma'], 'L0_xattn_ln_beta': _L0_xattn_in['ln_beta'], 'L0_ffn_router_w': _L0_ffn_in['router_w'], 'L0_ffn_gate_w': _L0_ffn_in['gate_w'], 'L0_ffn_up_w': _L0_ffn_in['up_w'], 'L0_ffn_down_w': _L0_ffn_in['down_w'], 'L1_xattn_W': _L1_xattn_in['W'], 'L1_xattn_b': _L1_xattn_in['b'], 'L1_ffn_gate_w': _L1_ffn_in['gate_w'], 'L1_ffn_w1': _L1_ffn_in['w1'], 'L1_ffn_w2': _L1_ffn_in['w2'], 'L1_ffn_w3': _L1_ffn_in['w3'], 'L1_ffn_sw1': _L1_ffn_in['sw1'], 'L1_ffn_sw2': _L1_ffn_in['sw2'], 'L1_ffn_sw3': _L1_ffn_in['sw3']}

def reference(x, ctx_512, g_xattn, g_ffn, L0_xattn_W_k, L0_xattn_b_k, L0_xattn_ln_gamma, L0_xattn_ln_beta, L0_ffn_router_w, L0_ffn_gate_w, L0_ffn_up_w, L0_ffn_down_w, L1_xattn_W, L1_xattn_b, L1_ffn_gate_w, L1_ffn_w1, L1_ffn_w2, L1_ffn_w3, L1_ffn_sw1, L1_ffn_sw2, L1_ffn_sw3):
    import jax
    import jax.numpy as jnp

    def _L0_xattn_ref(p, k_v, W_k, b_k, ln_gamma, ln_beta):
        import jax, jax.numpy as jnp
        import numpy as np
        EPS = 1e-06
        IMAGE_DIMS = 256
        kv = k_v @ W_k.T + b_k
        out = jnp.einsum('bij,bjd->bid', p, kv)
        scale = IMAGE_DIMS ** (-0.5)
        sim = jnp.einsum('bid,bjd->bij', out, kv) * scale
        mu = jnp.mean(sim, axis=-1, keepdims=True)
        var = jnp.var(sim, axis=-1, keepdims=True)
        sim = (sim - mu) * jax.lax.rsqrt(var + EPS) * ln_gamma + ln_beta
        attn = jax.nn.softmax(sim, axis=-1)
        return attn

    def _L0_ffn_ref(x, router_w, gate_w, up_w, down_w):
        import jax, jax.numpy as jnp
        import numpy as np
        B, S, H, F, E, K = (2, 128, 256, 688, 8, 2)
        b, s, h = x.shape
        xf = x.reshape(-1, h)
        logits = xf @ router_w.T
        top_v, top_i = jax.lax.top_k(logits, K)
        probs = jax.nn.softmax(top_v.astype(jnp.float32), axis=-1).astype(logits.dtype)
        combine = jnp.sum(jax.nn.one_hot(top_i, E, dtype=x.dtype) * probs[..., None], axis=1)
        g = jnp.einsum('th,efh->etf', xf, gate_w)
        u = jnp.einsum('th,efh->etf', xf, up_w)
        y = jnp.einsum('etf,ehf->eth', jax.nn.silu(g) * u, down_w)
        out = jnp.einsum('te,eth->th', combine, y)
        return out.reshape(b, s, h)

    def _L1_xattn_ref(x, adj, W, b):
        import jax, jax.numpy as jnp
        import numpy as np
        P_ASEM = 0.6
        D = x.shape[-1]
        Wi = W[:, :D]
        Wj = W[:, D:]
        si = jnp.einsum('bnd,d->bn', x, Wi[0])
        sj = jnp.einsum('bnd,d->bn', x, Wj[0])
        xij = jax.nn.sigmoid(si[:, :, None] + sj[:, None, :] + b[0])
        return P_ASEM * xij + (1.0 - P_ASEM) * adj

    def _L1_ffn_ref(x, gate_w, w1, w2, w3, sw1, sw2, sw3):
        import jax, jax.numpy as jnp
        import numpy as np
        DIM = 256
        INTER = 176
        N_ROUTED = 15
        TOPK = 2
        SHARED_INTER = 176

        def _swiglu(x, wa, wb, wo):
            return jax.nn.silu(x @ wa.T) * (x @ wb.T) @ wo.T
        shape = x.shape
        xf = x.reshape(-1, shape[-1])
        T = xf.shape[0]
        probs = jax.nn.softmax(xf @ gate_w.T, axis=-1)
        weights, indices = jax.lax.top_k(probs, TOPK)
        combine = jnp.zeros((T, N_ROUTED), xf.dtype).at[jnp.arange(T)[:, None], indices].add(weights)
        y = jnp.zeros_like(xf)
        for i in range(N_ROUTED):
            y = y + _swiglu(xf, w1[i], w3[i], w2[i]) * combine[:, i:i + 1]
        z = _swiglu(xf, sw1, sw3, sw2)
        return (y + z).reshape(shape)
    x = x + jnp.tanh(g_xattn[0]) * _L0_xattn_ref(_layernorm(x, axis=-1), ctx_512, L0_xattn_W_k, L0_xattn_b_k, L0_xattn_ln_gamma, L0_xattn_ln_beta)
    x = x + jnp.tanh(g_ffn[0]) * _L0_ffn_ref(_layernorm(x, axis=-1), L0_ffn_router_w, L0_ffn_gate_w, L0_ffn_up_w, L0_ffn_down_w)
    x = x + jnp.tanh(g_xattn[1]) * _L1_xattn_ref(ctx_512, _layernorm(x, axis=-1), L1_xattn_W, L1_xattn_b)
    x = x + jnp.tanh(g_ffn[1]) * _L1_ffn_ref(_layernorm(x, axis=-1), L1_ffn_gate_w, L1_ffn_w1, L1_ffn_w2, L1_ffn_w3, L1_ffn_sw1, L1_ffn_sw2, L1_ffn_sw3)
    return x

_drawn_inputs = setup_inputs


def setup_inputs(seed=0):
    import zlib

    import numpy as np

    out = dict(_drawn_inputs(seed))
    spreads = {'g_ffn': (-1.0, 0.6),
     'L0_xattn_b_k': (0.0, 0.8),
     'L0_xattn_ln_gamma': (1.0, 0.6),
     'L0_xattn_ln_beta': (0.0, 0.8)}
    factors = {'L0_xattn_W_k': 8.0,
     'L0_ffn_router_w': 4.755,
     'L0_ffn_gate_w': 4.163,
     'L0_ffn_up_w': 4.131,
     'L0_ffn_down_w': 4.135,
     'L1_ffn_gate_w': 8.0,
     'L1_ffn_w1': 8.0,
     'L1_ffn_w2': 8.0,
     'L1_ffn_w3': 8.0,
     'L1_ffn_sw1': 3.402,
     'L1_ffn_sw2': 3.371,
     'L1_ffn_sw3': 3.353}
    for name, (base, spread) in spreads.items():
        noise = np.random.default_rng([zlib.crc32(name.encode()), seed]).standard_normal(out[name].shape)
        drawn = base * np.exp(spread * noise) if base else spread * noise
        out[name] = jnp.asarray(drawn.astype(out[name].dtype))
    for name, factor in factors.items():
        out[name] = (out[name] * factor).astype(out[name].dtype)
    return out
```

```python
import concourse.bass as bass
from concourse import mybir
from contextlib import ExitStack

P = 128
B, N, H, D = 4, 256, 256, 64
T = B * N
NT = T // P
KH = H // P
E0, F0 = 8, 688
E1, F1 = 15, 176
SHARED = 0


def most_tiles(experts):
    return min(experts * (T // P), (2 * T + (P - 1) * experts) // P)


S0, S1 = most_tiles(E0), most_tiles(E1)
KF0 = [(j, min(P, F0 - j * P)) for j in range(-(-F0 // P))]
KF1 = [(j, min(P, F1 - j * P)) for j in range(-(-F1 // P))]
CH0 = F0 // 2
GU0, GU1 = KH * 2 * F0, KH * 2 * F1
WD0, WD1 = len(KF0) * H, len(KF1) * H
GUALL = E0 * GU0
WDALL = E0 * WD0



def second_weights():
    had_gu = had_dn = 0
    for k in range(1, E0):
        gu, dn = min(E1 + 1, k * GU0 // GU1), min(E1 + 1, k * WD0 // WD1)
        if gu > had_gu or dn > had_dn:
            yield k, had_gu, gu, had_dn, dn
        had_gu, had_dn = gu, dn


C_ID = 0
C_DESC = C_ID + P
C_THR = C_DESC + 16
C_LT = C_THR + NT - 1
C_SLOT = C_LT + E1 * E1
C_NH = C_SLOT + S1
C_ALL = C_NH + 1

M_CTX = 0
M_WK = M_CTX + T
M_WJ = M_WK + D
M_WI = M_WJ + P
M_ALL = M_WI + 1
M_ROWS = 80

V_GAMMA, V_BETA, V_GX, V_GF = 0, N, 2 * N, 2 * N + 2
V_ALL = 2 * N + 4

LN_EPS = 1e-5
SIM_EPS = 1e-6
SIM_SCALE = float(N) ** -0.5
NEVER = -3.0e38


def build(nc, x, small, vecs, router, const_f, const_b, gu0, wd0a, wd0b, gu1, wd1a, wd1b, out):
    fp32, bf16, i32 = mybir.dt.float32, mybir.dt.bfloat16, mybir.dt.int32
    ALU = mybir.AluOpType
    ACT = mybir.ActivationFunctionType
    X = mybir.AxisListType.X

    slots = nc.dram_tensor("slots", (S1 * P, H), fp32).ap()
    y_slots = nc.dram_tensor("y_slots", (S1 * P, H), fp32).ap()
    x_t = x.rearrange("(i p) h -> p i h", p=P)
    out_t = out.rearrange("(i p) h -> p i h", p=P)

    ctx = ExitStack()
    with ctx:
        def sb(name, shape, dt=fp32):
            return ctx.enter_context(nc.sbuf_tensor(name, shape, dt))

        def sem(name):
            return ctx.enter_context(nc.semaphore(name))

        wgu = sb("wgu", [P, GUALL])
        wdn = sb("wdn", [P, WDALL])
        xs = sb("xs", [P, NT, H])
        xn = sb("xn", [P, NT, H])
        edge = sb("edge", [P, NT, H])
        small_sb = sb("small_sb", [M_ROWS, M_ALL])
        vec_sb = sb("vec_sb", [P, V_ALL])
        router_sb = sb("router_sb", [P, KH, E0 + E1])
        cf = sb("cf", [P, C_ALL])
        cb = sb("cb", [P, 2 * P], bf16)
        zeros = sb("zeros", [P, H])
        gamma16 = sb("gamma16", [P, N])
        tg = sb("tg", [P, 4])
        edge_c = sb("edge_c", [P, 2])
        kvT = sb("kvT", [D, T])
        kv = sb("kv", [P, NT, D])
        half_si = sb("half_si", [P, NT])
        half_b = sb("half_b", [P, NT])
        pT = sb("pT", [P, 2, H])
        oT = sb("oT", [D, 2, P])
        z = sb("z", [P, 2, N])
        e = sb("e", [P, 2, N])
        st = sb("st", [P, NT, 6])
        mv = sb("mv", [P, NT, 2])
        ve = sb("ve", [P, NT])
        rs = sb("rs", [P, NT])
        mx = sb("mx", [P, NT])
        nmx = sb("nmx", [P, NT])
        sm = sb("sm", [P, NT])
        rc = sb("rc", [P, NT])
        cc = sb("cc", [P, NT])
        x_in = sb("x_in", [P, 2, H])
        xT = sb("xT", [P, 2, H])
        th = sb("th", [P, F0])
        hh = sb("hh", [P, F0])
        hT = sb("hT", [P, len(KF0) * P])
        y_sb = sb("y_sb", [P, 2, H])
        free = (E1 + 1) * GU1
        y_got = wgu[:, free:free + 2 * NT * H].rearrange("p (i h) -> p i h", h=H)
        xnT = wgu[:, free + 2 * NT * H:free + 3 * NT * H].rearrange("p (i h) -> p i h", h=H)

        psum = [ctx.enter_context(nc.psum_tensor(f"bank{i}", [P, 512], fp32)) for i in range(8)]
        ident = cf[:, C_ID:C_ID + P]

        x_here = [sem(f"x_here{i}") for i in range(B)]
        small_here, vec_here, router_here = sem("small_here"), sem("vec_here"), sem("router_here")
        const_here, constb_here = sem("const_here"), sem("constb_here")
        w0_here = [sem(f"w0_here{i}") for i in range(E0)]
        w1_here = [sem(f"w1_here{i}") for i, _ in enumerate(second_weights())]
        out_stored = sem("out_stored")
        zeroed, slots_zeroed = sem("zeroed"), sem("slots_zeroed")
        kvT_done, kv_done, kvT_copied, kv_copied = sem("kvT_done"), sem("kv_done"), sem("kvT_copied"), sem("kv_copied")
        gates_done = sem("gates_done")
        p_var, p_rstd, p_ready = sem("p_var"), sem("p_rstd"), sem("p_ready")
        pT_done, pT_copied = sem("pT_done"), sem("pT_copied")
        oT_done, oT_copied, sim_done = sem("oT_done"), sem("oT_copied"), sem("sim_done")
        s_var, s_rstd, z_ready, exp_done = sem("s_var"), sem("s_rstd"), sem("z_ready"), sem("exp_done")
        dve_step = sem("dve_step")
        act_step = sem("act_step")
        pool_step = sem("pool_step")
        sj_done, si_done, si_copied, edge_th, edge_c_ready, edge_ready = (
            sem("sj_done"), sem("si_done"), sem("si_copied"), sem("edge_th"), sem("edge_c_ready"), sem("edge_ready"))

        class Mixture:

            def __init__(m, n, experts, tiles, kf, chunk, ahead):
                m.split = 4 if n == 0 else 1
                m.n, m.E, m.S, m.kf, m.ahead = n, experts, tiles, kf, ahead
                m.logits = psum[7][:, 0:NT * experts].rearrange("p (i e) -> p i e", e=experts)
                m.ranks = psum[6][:, 256:256 + (NT + 1) * experts].rearrange("p (i e) -> p i e", e=experts)
                if n == 1:
                    m.logits = psum[5][:, 0:NT * experts].rearrange("p (i e) -> p i e", e=experts)
                m.var, m.rstd, m.xn_ready = sem(f"var{n}"), sem(f"rstd{n}"), sem(f"xn_ready{n}")
                m.xnT_done, m.xnT_copied = sem(f"xnT_done{n}"), sem(f"xnT_copied{n}")
                m.logits_done, m.picked = sem(f"logits_done{n}"), sem(f"picked{n}")
                m.shifted, m.exps = sem(f"shifted{n}"), sem(f"exps{n}")
                m.ranks_done = sem(f"ranks_done{n}")
                m.places_ready, m.experts_ready = sem(f"places_ready{n}"), sem(f"experts_ready{n}")
                m.scattered = sem(f"scattered{n}")
                m.x_loaded = [sem(f"x_loaded{n}{r}") for r in range(2)]
                m.xT_done, m.xT_copied = sem(f"xT_done{n}"), sem(f"xT_copied{n}")
                m.gu_done, m.th_done, m.h_made = sem(f"gu_done{n}"), sem(f"th_done{n}"), sem(f"h_made{n}")
                m.hT_done = sem(f"hT_done{n}")
                m.hT_copied_a, m.hT_copied_v = sem(f"hT_copied_a{n}"), sem(f"hT_copied_v{n}")
                m.y_done, m.y_copied = sem(f"y_done{n}"), sem(f"y_copied{n}")
                m.y_stored = [sem(f"y_stored{n}{r}") for r in range(2)]
                m.gathered = [sem(f"gathered{n}{i}") for i in range(NT)]
                m.x_new = sem(f"x_new{n}")
                m.half, m.z_added = sem(f"half{n}"), sem(f"z_added{n}")
                m.L = sb(f"L{n}", [P, NT, experts])
                m.w = sb(f"w{n}", [P, NT, experts])
                m.oh1 = sb(f"oh1{n}", [P, NT, experts])
                m.oh2 = sb(f"oh2{n}", [P, NT, experts])
                m.L2 = sb(f"L2{n}", [P, NT, experts])
                m.A = sb(f"A{n}", [P, NT + 1, experts], bf16)
                m.v1, m.v2, m.m = sb(f"v1{n}", [P, NT]), sb(f"v2{n}", [P, NT]), sb(f"m{n}", [P, NT])
                m.d, m.ed = sb(f"d{n}", [P, NT]), sb(f"ed{n}", [P, NT])
                m.den, m.p1 = sb(f"den{n}", [P, NT]), sb(f"p1{n}", [P, NT])
                m.c1, m.c2 = sb(f"c1{n}", [P, NT]), sb(f"c2{n}", [P, NT])
                m.cmp = sb(f"cmp{n}", [P, experts, NT - 1])
                m.tl, m.base, m.incl = sb(f"tl{n}", [P, experts]), sb(f"base{n}", [P, experts]), sb(f"incl{n}", [P, experts])
                m.lt = sb(f"lt{n}", [P, experts, experts])
                m.R2 = sb(f"R2{n}", [P, NT, experts])
                m.place = [sb(f"place{k}{n}", [P, NT], i32) for k in (1, 2)]
                m.scmp = sb(f"scmp{n}", [1, tiles, experts - 1])
                m.ownf = sb(f"ownf{n}", [1, tiles])
                m.owner = sb(f"owner{n}", [1, tiles], i32)

        mix = [Mixture(0, E0, S0, KF0, CH0, 1), Mixture(1, E1, S1, KF1, F1, 2)]

        def steps(eng, step, total, full):
            step(0, 0)
            step(1, 1)
            pairs = full // 2
            with eng.Fori(1, pairs) as j:
                step(j * 2, 0)
                step(j * 2 + 1, 1)
            for s in range(2 * pairs, total):
                step(s, s % 2)

        def since(eng, semaphore, value):
            if not isinstance(value, int) or value > 0:
                eng.wait_ge(semaphore, value)

        def below(s, limit):
            return not isinstance(s, int) or s < limit

        block = ctx.enter_context(nc.Block())

        @block.sync
        def _(sp):
            for b in range(B):
                sp.dma_start(xs[:, 2 * b:2 * b + 2, :], x_t[:, 2 * b:2 * b + 2, :]).then_inc(x_here[b], 16)
            sp.dma_start(router_sb[:], router).then_inc(router_here, 16)
            sp.dma_start(cb[:], const_b).then_inc(constb_here, 16)
            for n in range(E0):
                sp.dma_start(wgu[:, n * GU0:(n + 1) * GU0], gu0[n]).then_inc(w0_here[n], 16)
                tail = KF0[-1][0] * H
                sp.dma_start(wdn[:, n * WD0:n * WD0 + tail], wd0a[n]).then_inc(w0_here[n], 16)
                sp.dma_start(wdn[0:KF0[-1][1], n * WD0 + tail:(n + 1) * WD0], wd0b[n]).then_inc(w0_here[n], 16)
                if n == 2:
                    sp.wait_ge(zeroed, 1)
                    for part in range(3):
                        a, z_ = part * S1 // 3, (part + 1) * S1 // 3
                        sp.dma_start(slots[a * P:z_ * P, :].rearrange("(n p) h -> p n h", p=P),
                                     zeros[:].unsqueeze(1).to_broadcast([P, z_ - a, H])).then_inc(slots_zeroed, 16)

            for m in mix:
                def load(t, r):
                    if below(t, 2) and isinstance(t, int) and t < 2:
                        pass
                    else:
                        sp.wait_ge(m.xT_done, t - 1)
                    row = t * P
                    sp.dma_start(x_in[:, r, :], slots[bass.ds(row, P), :]).then_inc(m.x_loaded[r], 16)

                def store(s, r):
                    sp.wait_ge(m.y_copied, s + 1)
                    sp.dma_start(y_slots[bass.ds(s * P, P), :], y_sb[:, r, :]).then_inc(m.y_stored[r], 16)

                sp.wait_ge(m.scattered, 2 * NT * 16)
                lead = m.ahead + 3
                for t in range(lead):
                    load(t, t % 2)

                def step(s, r):
                    if below(s, m.S - lead):
                        load(s + lead, (r + lead) % 2)
                    store(s, r)

                steps(sp, step, m.S, m.S - lead)
            for i in range(NT):
                sp.wait_ge(mix[1].x_new, i + 1)
                sp.dma_start(out_t[:, i, :], xs[:, i, :]).then_inc(out_stored, 16)
            sp.wait_ge(out_stored, 16 * NT)

        @block.gpsimd
        def _(pool):
            nc.gpsimd.memset(zeros[:], 0.0).then_inc(zeroed, 1)
            minus_half = cf[:, C_NH:C_NH + 1]
            pool.wait_ge(const_here, 16)
            for i in range(NT):
                pool.wait_ge(p_var, i + 1)
                nc.gpsimd.tensor_tensor(rs[:, i:i + 1], ve[:, i:i + 1], minus_half, ALU.pow).then_inc(p_rstd, 1)

            def score_rstd(i):
                pool.wait_ge(s_var, i + 1)
                nc.gpsimd.tensor_tensor(rs[:, i:i + 1], ve[:, i:i + 1], minus_half, ALU.pow).then_inc(s_rstd, 1)

            def x_rstd(m, i):
                pool.wait_ge(m.var, i + 1)
                nc.gpsimd.tensor_tensor(rs[:, i:i + 1], ve[:, i:i + 1], minus_half, ALU.pow).then_inc(m.rstd, 1)

            score_rstd(0)
            for i in range(NT):
                if i + 1 < NT:
                    score_rstd(i + 1)
                x_rstd(mix[0], i)

            def scatter(m):
                pool.wait_ge(m.places_ready, 1)
                pool.wait_ge(m.xn_ready, NT)
                for i in range(NT):
                    for k in range(2):
                        nc.gpsimd.indirect_dma_start(
                            out=slots, out_offset=bass.IndirectOffsetOnAxis(ap=m.place[k][:, i:i + 1], axis=0),
                            in_=xn[:, i, :], in_offset=None).then_inc(m.scattered, 16)

            def gather(m):
                pool.wait_ge(m.y_stored[0], 16 * ((m.S + 1) // 2))
                pool.wait_ge(m.y_stored[1], 16 * (m.S // 2))
                for i in range(NT):
                    for k in range(2):
                        nc.gpsimd.indirect_dma_start(
                            out=y_got[:, 2 * i + k, :], out_offset=None, in_=y_slots[0:m.S * P, :],
                            in_offset=bass.IndirectOffsetOnAxis(ap=m.place[k][:, i:i + 1], axis=0),
                        ).then_inc(m.gathered[i], 16)

            pool.wait_ge(slots_zeroed, 16 * 3)
            scatter(mix[0])
            pool.wait_ge(edge_c_ready, 1)
            for i in range(NT):
                pool.wait_ge(edge_th, i + 1)
                nc.gpsimd.tensor_scalar(edge[:, i, :], edge[:, i, :], edge_c[:, 0:1], edge_c[:, 0:1],
                                        ALU.mult, ALU.add).then_inc(edge_ready, 1)
            for n, (k, gu_a, gu_z, dn_a, dn_z) in enumerate(second_weights()):
                pool.wait_ge(mix[0].y_done, most_tiles(k))
                if gu_z > gu_a:
                    nc.gpsimd.dma_start(
                        wgu[:, gu_a * GU1:gu_z * GU1].rearrange("p (e n) -> p e n", n=GU1),
                        gu1[gu_a:gu_z].rearrange("e p n -> p e n")).then_inc(w1_here[n], 16)
                if dn_z > dn_a:
                    dn = wdn[:, dn_a * WD1:dn_z * WD1].rearrange("p (e n) -> p e n", n=WD1)
                    nc.gpsimd.dma_start(dn[:, :, 0:H], wd1a[dn_a:dn_z].rearrange("e p n -> p e n")
                                        ).then_inc(w1_here[n], 16)
                    nc.gpsimd.dma_start(dn[0:KF1[1][1], :, H:2 * H], wd1b[dn_a:dn_z].rearrange("e p n -> p e n")
                                        ).then_inc(w1_here[n], 16)
            gather(mix[0])
            for i in range(NT):
                pool.wait_ge(p_var, NT + i + 1)
                nc.gpsimd.tensor_tensor(rs[:, i:i + 1], ve[:, i:i + 1], minus_half, ALU.pow).then_inc(p_rstd, 1)
                x_rstd(mix[1], i)
            scatter(mix[1])
            gather(mix[1])

        @block.scalar
        def _(act):
            act.dma_start(cf[:], const_f).then_inc(const_here, 16)
            act.dma_start(small_sb[:], small).then_inc(small_here, 16)
            act.dma_start(vec_sb[:], vecs.to_broadcast([P, V_ALL])).then_inc(vec_here, 16)
            act.wait_ge(vec_here, 16)
            nc.scalar.activation(tg[:], vec_sb[:, V_GX:V_GX + 4], ACT.Tanh).then_inc(gates_done, 1)
            for h in range(2):
                act.wait_ge(kvT_done, h + 1)
                nc.scalar.activation(kvT[:, h * 512:(h + 1) * 512], psum[4 + h][0:D, :], ACT.Copy).then_inc(kvT_copied, 1)
            act.wait_ge(kv_done, 1)
            nc.scalar.activation(kv[:].rearrange("p i d -> p (i d)"), psum[6][:, :], ACT.Copy).then_inc(kv_copied, 1)

            def copy_pT(i):
                act.wait_ge(pT_done, i + 1)
                since(act, oT_done, i - 1)
                nc.scalar.activation(pT[:, i % 2, :], psum[i % 2][:, 0:H], ACT.Copy).then_inc(pT_copied, 1)

            def copy_oT(i):
                act.wait_ge(oT_done, i + 1)
                since(act, sim_done, i - 1)
                nc.scalar.activation(oT[:, i % 2, :], psum[2 + i % 2][0:D, 0:P], ACT.Copy).then_inc(oT_copied, 1)

            def exp(i):
                act.wait_ge(z_ready, i + 1)
                nc.scalar.activation(e[:, i % 2, :], z[:, i % 2, :], ACT.Exp, bias=nmx[:, i:i + 1],
                                     accum_out=sm[:, i:i + 1]).then_inc(exp_done, 1)

            def copy_xnT(m, i, dst):
                act.wait_ge(m.xnT_done, i + 1)
                nc.scalar.activation(dst, psum[6][:, 0:H], ACT.Copy).then_inc(m.xnT_copied, 1)

            copy_pT(0)
            copy_pT(1)
            copy_oT(0)
            for i in range(NT):
                if i + 2 < NT:
                    copy_pT(i + 2)
                if i + 1 < NT:
                    copy_oT(i + 1)
                exp(i)
                if i >= 1:
                    copy_xnT(mix[0], i - 1, xT[:, (i - 1) % 2, :])
            copy_xnT(mix[0], NT - 1, xT[:, (NT - 1) % 2, :])

            def route_exps(m):
                act.wait_ge(m.shifted, 1)
                nc.scalar.activation(m.ed[:], m.d[:], ACT.Exp).then_inc(m.exps, 1)
                if m.n == 1:
                    nc.scalar.activation(m.L2[:].rearrange("p i e -> p (i e)"),
                                         m.L2[:].rearrange("p i e -> p (i e)"), ACT.Exp).then_inc(m.exps, 1)

            route_exps(mix[0])
            act.wait_ge(si_done, 1)
            nc.scalar.activation(half_si[:], psum[2][:, 0:NT], ACT.Copy, scale=0.5).then_inc(si_copied, 1)
            act.wait_ge(si_copied, 1)
            act.wait_ge(sj_done, 2)
            for i in range(NT):
                b = i // 2
                nc.scalar.activation(edge[:, i, :], psum[4 + b // 2][:, (b % 2) * N:(b % 2 + 1) * N], ACT.Tanh,
                                     bias=half_si[:, i:i + 1], scale=0.5).then_inc(edge_th, 1)

            def tanh_half(m, t, r):
                if m.n == 0:
                    for c in range(2):
                        act.wait_ge(m.gu_done, 2 * t + c + 1)
                        since(act, m.h_made, 2 * (t - 1) + c + 1)
                        nc.scalar.activation(th[:, c * CH0:(c + 1) * CH0], psum[2 * c][:, 0:CH0], ACT.Tanh,
                                             scale=0.5).then_inc(m.th_done, 1)
                else:
                    act.wait_ge(m.gu_done, t + 1)
                    since(act, m.h_made, t - 1)
                    nc.scalar.activation(th[:, r * F1:(r + 1) * F1], psum[r][:, 0:F1], ACT.Tanh,
                                         scale=0.5).then_inc(m.th_done, 1)

            def copy_hT(m, s, r):
                act.wait_ge(m.hT_done, s + 1)
                n = 512 if m.n == 0 else P
                nc.scalar.activation(hT[:, 0:n], psum[4][:, 0:n], ACT.Copy, scale=0.5).then_inc(m.hT_copied_a, 1)

            m = mix[0]
            tanh_half(m, 0, 0)

            def step0(s, r):
                copy_hT(m, s, r)
                if below(s, m.S - 1):
                    tanh_half(m, s + 1, (r + 1) % 2)
                act.wait_ge(m.y_done, s + 1)
                if not isinstance(s, int) or s >= 2:
                    act.wait_ge(m.y_stored[r], s * 8 - 8 * r)
                nc.scalar.activation(y_sb[:, r, :], psum[7][:, 0:H], ACT.Copy).then_inc(m.y_copied, 1)

            steps(act, step0, m.S, m.S - 1)

            m1 = mix[1]
            for i in range(NT):
                copy_xnT(m1, i, xnT[:, i, :])
            route_exps(m1)
            tanh_half(m1, 0, 0)
            tanh_half(m1, 1, 1)
            for i in range(NT):
                copy_hT(m1, i, i % 2)
                tanh_half(m1, i + 2, i % 2)

            def step1(s, r):
                copy_hT(m1, s + NT, r)
                if below(s, m1.S - 2):
                    tanh_half(m1, s + (NT + 2), r)
                act.wait_ge(m1.y_done, s + (NT + 1))
                if not isinstance(s, int) or s >= 2:
                    act.wait_ge(m1.y_stored[r], s * 8 - 8 * r)
                nc.scalar.activation(y_sb[:, r, :], psum[7][:, 0:H], ACT.Copy).then_inc(m1.y_copied, 1)

            steps(act, step1, m1.S, m1.S - 2)

        @block.vector
        def _(dve):
            count = [0]

            def then(instruction):
                count[0] += 1
                instruction.then_inc(dve_step, 1)
                dve.wait_ge(dve_step, count[0])

            def stats(src, i, eps, scale, signal):
                then(nc.vector.bn_stats(st[:, i, :], src))
                then(nc.vector.bn_aggr(mv[:, i, :], st[:, i, :]))
                nc.vector.tensor_scalar(ve[:, i:i + 1], mv[:, i, 1:2], scale, eps, ALU.mult, ALU.add).then_inc(signal, 1)

            for i in range(NT + 1):
                if i < NT:
                    if i % 2 == 0:
                        dve.wait_ge(x_here[i // 2], 16)
                    stats(xs[:, i, :], i, LN_EPS, 1.0, p_var)
                if i >= 1:
                    dve.wait_ge(p_rstd, i)
                    nc.vector.tensor_scalar(xn[:, i - 1, :], xs[:, i - 1, :], mv[:, i - 1, 0:1], rs[:, i - 1:i],
                                            ALU.subtract, ALU.mult).then_inc(p_ready, 1)
            dve.wait_ge(vec_here, 16)
            dve.wait_ge(gates_done, 1)
            nc.vector.tensor_scalar(edge_c[:, 0:1], tg[:, 1:2], 0.3, None, ALU.mult).then_inc(edge_c_ready, 1)
            nc.vector.tensor_scalar(edge_c[:, 1:2], tg[:, 1:2], 0.4, None, ALU.mult)
            for m in mix:
                nc.vector.memset(m.A[:, NT, :], 0.0)
            then(nc.vector.tensor_scalar(gamma16[:], vec_sb[:, V_GAMMA:V_GAMMA + N], SIM_SCALE, None, ALU.mult))

            def score_stats(i):
                dve.wait_ge(sim_done, i + 1)
                stats(psum[4 + i % 2][:, 0:N], i, SIM_EPS, SIM_SCALE * SIM_SCALE, s_var)

            def score_norm(i):
                r = i % 2
                dve.wait_ge(s_rstd, i + 1)
                then(nc.vector.tensor_scalar(z[:, r, :], psum[4 + r][:, 0:N], mv[:, i, 0:1], rs[:, i:i + 1],
                                             ALU.subtract, ALU.mult))
                then(nc.vector.tensor_tensor(z[:, r, :], z[:, r, :], gamma16[:], ALU.mult))
                then(nc.vector.tensor_tensor_reduce(out=z[:, r, :], in0=z[:, r, :], in1=vec_sb[:, V_BETA:V_BETA + N],
                                                    scale=1.0, scalar=NEVER, op0=ALU.add, op1=ALU.max,
                                                    accum_out=mx[:, i:i + 1]))
                nc.vector.tensor_scalar(nmx[:, i:i + 1], mx[:, i:i + 1], -1.0, None, ALU.mult).then_inc(z_ready, 1)

            def attend(i):
                dve.wait_ge(exp_done, i + 1)
                then(nc.vector.reciprocal(rc[:, i:i + 1], sm[:, i:i + 1]))
                then(nc.vector.tensor_tensor(cc[:, i:i + 1], rc[:, i:i + 1], tg[:, 0:1], ALU.mult))
                then(nc.vector.scalar_tensor_tensor(out=xs[:, i, :], in0=e[:, i % 2, :], scalar=cc[:, i:i + 1],
                                                    in1=xs[:, i, :], op0=ALU.mult, op1=ALU.add))
                stats(xs[:, i, :], i, LN_EPS, 1.0, mix[0].var)

            def x_norm(m, i):
                dve.wait_ge(m.rstd, i + 1)
                nc.vector.tensor_scalar(xn[:, i, :], xs[:, i, :], mv[:, i, 0:1], rs[:, i:i + 1],
                                        ALU.subtract, ALU.mult).then_inc(m.xn_ready, 1)

            score_stats(0)
            for i in range(NT):
                score_norm(i)
                if i + 1 < NT:
                    score_stats(i + 1)
                attend(i)
                x_norm(mix[0], i)

            def route(m):
                E = m.E
                desc = cf[:, C_DESC:C_DESC + E].unsqueeze(1).to_broadcast([P, NT, E])
                lt = cf[:, C_LT:C_LT + E1 * E1].rearrange("p (a b) -> p a b", a=E1)[:, 0:E, 0:E]

                def wide(v):
                    return v.unsqueeze(2).to_broadcast([P, NT, E])

                def first_best(logits, best, onehot):
                    then(nc.vector.tensor_reduce(out=best[:], in_=logits[:], axis=X, op=ALU.max))
                    then(nc.vector.tensor_tensor(m.w[:], logits[:], wide(best[:]), ALU.is_equal))
                    then(nc.vector.tensor_tensor(m.w[:], m.w[:], desc, ALU.mult))
                    then(nc.vector.tensor_reduce(out=m.m[:], in_=m.w[:], axis=X, op=ALU.max))
                    then(nc.vector.tensor_tensor(onehot[:], m.w[:], wide(m.m[:]), ALU.is_equal))

                dve.wait_ge(m.logits_done, NT)
                then(nc.vector.tensor_copy(m.L[:], m.logits))
                first_best(m.L, m.v1, m.oh1)
                then(nc.vector.scalar_tensor_tensor(out=m.L2[:], in0=m.oh1[:], scalar=NEVER, in1=m.L[:],
                                                    op0=ALU.mult, op1=ALU.add))
                first_best(m.L2, m.v2, m.oh2)
                nc.vector.tensor_tensor(m.A[:, 0:NT, :], m.oh1[:], m.oh2[:], ALU.add).then_inc(m.picked, 1)
                if m.n == 1:
                    nc.vector.tensor_tensor(m.L2[:], m.L[:], wide(m.v1[:]), ALU.subtract)
                nc.vector.tensor_tensor(m.d[:], m.v2[:], m.v1[:], ALU.subtract).then_inc(m.shifted, 1)

                dve.wait_ge(m.ranks_done, 1)
                then(nc.vector.tensor_tensor(
                    m.cmp[:], m.ranks[:, NT, :].unsqueeze(2).to_broadcast([P, E, NT - 1]),
                    cf[:, C_THR:C_THR + NT - 1].unsqueeze(1).to_broadcast([P, E, NT - 1]), ALU.is_gt))
                then(nc.vector.tensor_reduce(out=m.tl[:], in_=m.cmp[:], axis=X, op=ALU.add))
                then(nc.vector.tensor_scalar(m.tl[:], m.tl[:], 1.0, None, ALU.add))
                then(nc.vector.tensor_tensor(m.lt[:], lt, m.tl[:].unsqueeze(1).to_broadcast([P, E, E]), ALU.mult))
                then(nc.vector.tensor_reduce(out=m.base[:], in_=m.lt[:], axis=X, op=ALU.add))
                then(nc.vector.scalar_tensor_tensor(
                    out=m.R2[:], in0=m.base[:].unsqueeze(1).to_broadcast([P, NT, E]), scalar=float(P),
                    in1=m.ranks[:, 0:NT, :], op0=ALU.mult, op1=ALU.add))
                then(nc.vector.tensor_tensor(m.w[:], m.R2[:], m.oh1[:], ALU.mult))
                then(nc.vector.tensor_reduce(out=m.v2[:], in_=m.w[:], axis=X, op=ALU.add))
                then(nc.vector.tensor_copy(m.place[0][:], m.v2[:]))
                then(nc.vector.tensor_tensor(m.w[:], m.R2[:], m.oh2[:], ALU.mult))
                then(nc.vector.tensor_reduce(out=m.v2[:], in_=m.w[:], axis=X, op=ALU.add))
                nc.vector.tensor_copy(m.place[1][:], m.v2[:]).then_inc(m.places_ready, 1)
                then(nc.vector.tensor_tensor(m.incl[:], m.base[:], m.tl[:], ALU.add))
                then(nc.vector.tensor_tensor(
                    m.scmp[:], cf[0:1, C_SLOT:C_SLOT + m.S].unsqueeze(2).to_broadcast([1, m.S, E - 1]),
                    m.incl[0:1, 0:E - 1].unsqueeze(1).to_broadcast([1, m.S, E - 1]), ALU.is_ge))
                then(nc.vector.tensor_reduce(out=m.ownf[:], in_=m.scmp[:], axis=X, op=ALU.add))
                nc.vector.tensor_copy(m.owner[:], m.ownf[:]).then_inc(m.experts_ready, 1)
                dve.wait_ge(m.exps, m.n + 1)
                if m.n == 0:
                    then(nc.vector.tensor_scalar(m.den[:], m.ed[:], 1.0, None, ALU.add))
                else:
                    then(nc.vector.tensor_reduce(out=m.den[:], in_=m.L2[:], axis=X, op=ALU.add))
                then(nc.vector.reciprocal(m.p1[:], m.den[:]))
                then(nc.vector.tensor_scalar(m.c1[:], m.p1[:], tg[:, 2 + m.n:3 + m.n], None, ALU.mult))
                then(nc.vector.tensor_tensor(m.c2[:], m.c1[:], m.ed[:], ALU.mult))

            route(mix[0])

            def copy_hT(m, s, r):
                dve.wait_ge(m.hT_done, s + 1)
                if m.n == 0:
                    nc.vector.tensor_scalar(hT[:, 512:640], psum[5][:, 0:P], 0.5, None, ALU.mult)
                    nc.vector.tensor_scalar(hT[0:KF0[-1][1], 640:768], psum[5][0:KF0[-1][1], P:2 * P], 0.5, None,
                                            ALU.mult).then_inc(m.hT_copied_v, 1)
                else:
                    nc.vector.tensor_scalar(hT[0:KF1[-1][1], P:2 * P], psum[5][0:KF1[-1][1], 0:P], 0.5, None,
                                            ALU.mult).then_inc(m.hT_copied_v, 1)

            def hidden(m, t, r, half_step):
                if m.n == 0:
                    for c in range(2):
                        cols = slice(c * CH0, (c + 1) * CH0)
                        dve.wait_ge(m.th_done, 2 * t + c + 1)
                        nc.vector.scalar_tensor_tensor(out=hh[:, cols], in0=th[:, cols], scalar=1.0,
                                                       in1=psum[2 * c][:, 0:CH0], op0=ALU.add,
                                                       op1=ALU.mult).then_inc(half_step, 1)
                        dve.wait_ge(half_step, 2 * t + c + 1)
                        nc.vector.tensor_tensor(hh[:, cols], hh[:, cols], psum[2 * c + 1][:, 0:CH0],
                                                ALU.mult).then_inc(m.h_made, 1)
                else:
                    cols = slice(r * F1, (r + 1) * F1)
                    dve.wait_ge(m.th_done, t + 1)
                    since(dve, m.hT_done, t - 1)
                    nc.vector.scalar_tensor_tensor(out=hh[:, cols], in0=th[:, cols], scalar=1.0,
                                                   in1=psum[r][:, 0:F1], op0=ALU.add,
                                                   op1=ALU.mult).then_inc(half_step, 1)
                    dve.wait_ge(half_step, t + 1)
                    nc.vector.tensor_tensor(hh[:, cols], hh[:, cols], psum[r][:, F1:2 * F1],
                                            ALU.mult).then_inc(m.h_made, 1)

            def copy_xT(m, t, r):
                dve.wait_ge(m.xT_done, t + 1)
                nc.vector.tensor_copy(xT[:, r, :], psum[6][:, 0:H]).then_inc(m.xT_copied, 1)

            m = mix[0]
            copy_xT(m, 0, 0)
            hidden(m, 0, 0, m.half)
            copy_xT(m, 1, 1)

            def step0(s, r):
                copy_hT(m, s, r)
                if below(s, m.S - 1):
                    hidden(m, s + 1, (r + 1) % 2, m.half)
                if below(s, m.S - 2):
                    copy_xT(m, s + 2, r)

            steps(dve, step0, m.S, m.S - 2)

            def combine(m, i):
                dve.wait_ge(m.gathered[i], 32)
                then(nc.vector.scalar_tensor_tensor(out=xs[:, i, :], in0=y_got[:, 2 * i, :], scalar=m.c1[:, i:i + 1],
                                                    in1=xs[:, i, :], op0=ALU.mult, op1=ALU.add))
                return nc.vector.scalar_tensor_tensor(out=xs[:, i, :], in0=y_got[:, 2 * i + 1, :],
                                                      scalar=m.c2[:, i:i + 1], in1=xs[:, i, :],
                                                      op0=ALU.mult, op1=ALU.add)

            m1 = mix[1]
            for i in range(NT):
                then(combine(mix[0], i))
                stats(xs[:, i, :], i, LN_EPS, 1.0, p_var)
                dve.wait_ge(p_rstd, NT + i + 1)
                then(nc.vector.tensor_scalar(cc[:, i:i + 1], rs[:, i:i + 1], edge_c[:, 1:2], None, ALU.mult))
                then(nc.vector.tensor_scalar(xn[:, i, :], xs[:, i, :], mv[:, i, 0:1], cc[:, i:i + 1],
                                             ALU.subtract, ALU.mult))
                then(nc.vector.tensor_tensor(xs[:, i, :], xs[:, i, :], xn[:, i, :], ALU.add))
                if i == 0:
                    dve.wait_ge(edge_ready, NT)
                then(nc.vector.tensor_tensor(xs[:, i, :], xs[:, i, :], edge[:, i, :], ALU.add))
                stats(xs[:, i, :], i, LN_EPS, 1.0, m1.var)
                x_norm(m1, i)
            route(m1)

            hidden(m1, 0, 0, m1.half)
            hidden(m1, 1, 1, m1.half)
            for i in range(NT):
                copy_hT(m1, i, i % 2)
                hidden(m1, i + 2, i % 2, m1.half)
                if i >= NT - 3:
                    copy_xT(m1, i - (NT - 3), (i - (NT - 3)) % 2)
                dve.wait_ge(m1.y_done, i + 1)
                nc.vector.scalar_tensor_tensor(out=xs[:, i, :], in0=psum[7][:, 0:H], scalar=tg[:, 3:4],
                                               in1=xs[:, i, :], op0=ALU.mult, op1=ALU.add).then_inc(m1.z_added, 1)

            def step1(s, r):
                copy_hT(m1, s + NT, r)
                if below(s, m1.S - 2):
                    hidden(m1, s + (NT + 2), r, m1.half)
                if below(s, m1.S - 3):
                    copy_xT(m1, s + 3, (r + 1) % 2)

            steps(dve, step1, m1.S, m1.S - 3)
            for i in range(NT):
                combine(m1, i).then_inc(m1.x_new, 1)

        @block.tensor
        def _(pe):
            mm = nc.tensor.matmul

            def turn(dst, src):
                return nc.tensor.transpose(dst, src, cf[:, C_ID:C_ID + P])

            pe.wait_ge(small_here, 16)
            ctx_all = small_sb[0:D + 1, M_CTX:M_CTX + T]
            wk = small_sb[0:D + 1, M_WK:M_WK + D]
            for h in range(2):
                mm(psum[4 + h][0:D, :], wk, ctx_all[:, h * 512:(h + 1) * 512], start=True, stop=True).then_inc(kvT_done, 1)
            for i in range(NT):
                last = mm(psum[6][:, i * D:(i + 1) * D], ctx_all[:, i * P:(i + 1) * P], wk, start=True, stop=True)
            last.then_inc(kv_done, 1)
            pe.wait_ge(const_here, 16)

            def turn_p(i):
                pe.wait_ge(p_ready, i + 1)
                since(pe, pT_copied, i - 1)
                for k in range(KH):
                    last = turn(psum[i % 2][:, k * P:(k + 1) * P], xn[:, i, k * P:(k + 1) * P])
                last.then_inc(pT_done, 1)

            def attend(i):
                if i == 0:
                    pe.wait_ge(kv_copied, 1)
                pe.wait_ge(pT_copied, i + 1)
                since(pe, oT_copied, i - 1)
                for k in range(KH):
                    last = mm(psum[2 + i % 2][0:D, 0:P], kv[:, 2 * (i // 2) + k, :], pT[:, i % 2, k * P:(k + 1) * P],
                              start=(k == 0), stop=(k == KH - 1))
                last.then_inc(oT_done, 1)

            def score(i):
                if i == 0:
                    pe.wait_ge(kvT_copied, 2)
                pe.wait_ge(oT_copied, i + 1)
                since(pe, z_ready, i - 1)
                b = i // 2
                mm(psum[4 + i % 2][:, 0:N], oT[:, i % 2, :], kvT[:, b * N:(b + 1) * N], start=True,
                   stop=True).then_inc(sim_done, 1)

            def turn_xn(m, i):
                pe.wait_ge(m.xn_ready, i + 1)
                since(pe, m.xnT_copied, i)
                for k in range(KH):
                    last = turn(psum[6][:, k * P:(k + 1) * P], xn[:, i, k * P:(k + 1) * P])
                last.then_inc(m.xnT_done, 1)

            def logits(m, i, src):
                pe.wait_ge(m.xnT_copied, i + 1)
                rw = router_sb[:, :, 0:E0] if m.n == 0 else router_sb[:, :, E0:E0 + E1]
                for k in range(KH):
                    last = mm(m.logits[:, i, :], src[:, k * P:(k + 1) * P], rw[:, k, :],
                              start=(k == 0), stop=(k == KH - 1))
                last.then_inc(m.logits_done, 1)

            def ranks(m):
                pe.wait_ge(m.picked, 1)
                mm(m.ranks, cb[:, 0:P], m.A[:], start=True, stop=False)
                for i in range(NT):
                    last = mm(m.ranks[:, i + 1:NT + 1, :], cb[:, P:2 * P],
                              m.A[:, i:i + 1, :].to_broadcast([P, NT - i, m.E]), start=False, stop=(i == NT - 1))
                last.then_inc(m.ranks_done, 1)

            turn_p(0)
            turn_p(1)
            attend(0)
            pe.wait_ge(router_here, 16)
            for i in range(NT):
                if i + 2 < NT:
                    turn_p(i + 2)
                if i + 1 < NT:
                    attend(i + 1)
                score(i)
                if i >= 1:
                    turn_xn(mix[0], i - 1)
                    logits(mix[0], i - 1, xT[:, (i - 1) % 2, :])
            turn_xn(mix[0], NT - 1)
            logits(mix[0], NT - 1, xT[:, (NT - 1) % 2, :])
            pe.wait_ge(constb_here, 16)
            ranks(mix[0])
            wj = small_sb[0:D + 1, M_WJ:M_WJ + P]
            wi = small_sb[0:D + 1, M_WI:M_WI + 1]
            pe.wait_ge(z_ready, NT)
            for h in range(2):
                mm(psum[4 + h][:, :], wj, ctx_all[:, h * 512:(h + 1) * 512], start=True, stop=True).then_inc(sj_done, 1)
            for i in range(NT):
                last = mm(psum[2][:, i:i + 1], ctx_all[:, i * P:(i + 1) * P], wi, start=True, stop=True)
            last.then_inc(si_done, 1)

            def turn_x(m, t, r):
                if isinstance(t, int):
                    pe.wait_ge(m.x_loaded[r], 16 * (t // 2 + 1))
                else:
                    pe.wait_ge(m.x_loaded[r], t * 8 + (16 - 8 * r))
                since(pe, m.xT_copied, t)
                for k in range(KH):
                    last = turn(psum[6][:, k * P:(k + 1) * P], x_in[:, r, k * P:(k + 1) * P])
                last.then_inc(m.xT_done, 1)

            def turn_h(m, s, r):
                base = 0 if m.n == 0 else r * F1
                pe.wait_ge(m.h_made, (s + 1) * (2 if m.n == 0 else 1))
                for j, n in m.kf:
                    bank, col = (4, j * P) if j < m.split else (5, (j - m.split) * P)
                    last = nc.tensor.transpose(psum[bank][0:n, col:col + P],
                                               hh[:, base + j * P:base + j * P + n], cf[:, C_ID:C_ID + P])
                last.then_inc(m.hT_done, 1)

            def down(m, s, wd):
                pe.wait_ge(m.hT_copied_a, s + 1)
                pe.wait_ge(m.hT_copied_v, s + 1)
                for j, n in m.kf:
                    last = mm(psum[7][:, 0:H], hT[0:n, j * P:(j + 1) * P], wd(j, n),
                              start=(j == 0), stop=(j == len(m.kf) - 1))
                last.then_inc(m.y_done, 1)

            m = mix[0]

            def owner(m, t):
                return pe.value_load(m.owner[0:1, bass.ds(t, 1)], min_val=0, max_val=m.E - 1)

            def gate_up0(t, r):
                at = owner(m, t) * GU0
                pe.wait_ge(m.xT_copied, t + 1)
                for c in range(2):
                    since(pe, m.h_made, 2 * (t - 1) + c + 1)
                    for g in range(2):
                        for k in range(KH):
                            last = mm(psum[2 * c + g][:, 0:CH0], xT[:, r, k * P:(k + 1) * P],
                                      wgu[:, bass.ds(at + (k * 4 + 2 * c + g) * CH0, CH0)],
                                      start=(k == 0), stop=(k == KH - 1))
                    last.then_inc(m.gu_done, 1)

            def down0(s, r):
                at = owner(m, s) * WD0
                since(pe, m.y_copied, s)
                down(m, s, lambda j, n: wdn[0:n, bass.ds(at + j * H, H)])

            pe.wait_ge(edge_th, NT)
            pe.wait_ge(m.experts_ready, 1)
            turn_x(m, 0, 0)
            pe.wait_ge(w0_here[0], 48)
            gate_up0(0, 0)
            turn_x(m, 1, 1)

            def step0(s, r):
                turn_h(m, s, r)
                if isinstance(s, int) and s < 2:
                    for n in ([1] if s == 0 else range(2, E0)):
                        pe.wait_ge(w0_here[n], 48)
                if below(s, m.S - 1):
                    gate_up0(s + 1, (r + 1) % 2)
                down0(s, r)
                if below(s, m.S - 2):
                    turn_x(m, s + 2, r)

            steps(pe, step0, m.S, m.S - 2)

            m1 = mix[1]

            def gate_up1(t, r, src, at):
                since(pe, m1.h_made, t - 1)
                for k in range(KH):
                    last = mm(psum[r][:, 0:2 * F1], src[:, k * P:(k + 1) * P],
                              wgu[:, bass.ds(at + k * 2 * F1, 2 * F1)], start=(k == 0), stop=(k == KH - 1))
                last.then_inc(m1.gu_done, 1)

            def gate_up_slots(t, r):
                at = owner(m1, t) * GU1 + GU1
                pe.wait_ge(m1.xT_copied, t + 1)
                gate_up1(t + NT, r, xT[:, r, :], at)

            pe.wait_ge(mix[0].y_copied, S0)
            for i in range(NT):
                turn_xn(m1, i)
                logits(m1, i, xnT[:, i, :])
            for n, (_, gu_a, gu_z, dn_a, dn_z) in enumerate(second_weights()):
                pe.wait_ge(w1_here[n], 16 * (gu_z > gu_a) + 32 * (dn_z > dn_a))
            for i in range(2):
                gate_up1(i, i, xnT[:, i, :], SHARED)
            ranks(m1)
            for i in range(NT):
                turn_h(m1, i, i % 2)
                if i + 2 < NT:
                    gate_up1(i + 2, i % 2, xnT[:, i + 2, :], SHARED)
                else:
                    if i + 2 == NT:
                        pe.wait_ge(m1.experts_ready, 1)
                    gate_up_slots(i + 2 - NT, i % 2)
                since(pe, m1.z_added, i)
                down(m1, i, lambda j, n: wdn[0:n, j * H:(j + 1) * H])
                if i >= NT - 3:
                    turn_x(m1, i - (NT - 3), (i - (NT - 3)) % 2)

            def step1(s, r):
                turn_h(m1, s + NT, r)
                if below(s, m1.S - 2):
                    gate_up_slots(s + 2, r)
                if isinstance(s, int) and s == 0:
                    pe.wait_ge(m1.z_added, NT)
                at = owner(m1, s) * WD1 + WD1
                since(pe, m1.y_copied, s)
                down(m1, s + NT, lambda j, n: wdn[0:n, bass.ds(at + j * H, H)])
                if below(s, m1.S - 3):
                    turn_x(m1, s + 3, (r + 1) % 2)

            steps(pe, step1, m1.S, m1.S - 3)


def _constants():
    import numpy as np
    c = np.zeros((P, C_ALL), np.float32)
    c[:, C_ID:C_ID + P] = np.eye(P)
    c[:, C_DESC:C_DESC + 16] = 16 - np.arange(16)
    c[:, C_THR:C_THR + NT - 1] = P * np.arange(1, NT)
    c[:, C_LT:C_LT + E1 * E1] = np.tril(np.ones((E1, E1)), -1).ravel()
    c[:, C_SLOT:C_SLOT + S1] = np.arange(S1)
    c[:, C_NH] = -0.5
    return c, np.concatenate([np.triu(np.ones((P, P)), 1), np.ones((P, P))], 1)


def kernel(**inputs):
    import numpy as np
    import concourse.bacc as bacc
    from concourse.bass_utils import run_bass_kernel_spmd

    a = {k: np.asarray(v) for k, v in inputs.items()}
    f32 = np.float32
    const_f, const_b = _constants()

    small = np.zeros((M_ROWS, M_ALL), f32)
    small[0:D, M_CTX:M_CTX + T] = a["ctx_512"].reshape(T, D).T
    small[D, M_CTX:M_CTX + T] = 1.0
    small[0:D, M_WK:M_WK + D] = a["L0_xattn_W_k"].T
    small[D, M_WK:M_WK + D] = a["L0_xattn_b_k"]
    small[0:D, M_WJ:M_WJ + P] = a["L1_xattn_W"][0, D:, None]
    small[D, M_WJ:M_WJ + P] = a["L1_xattn_b"][0]
    small[0:D, M_WI] = a["L1_xattn_W"][0, :D]
    vecs = np.concatenate([a["L0_xattn_ln_gamma"], a["L0_xattn_ln_beta"], a["g_xattn"], a["g_ffn"]])[None]
    router = np.concatenate([a["L0_ffn_router_w"], a["L1_ffn_gate_w"]], 0).T.reshape(KH, P, E0 + E1)

    def split(w, halves):
        e, f, _ = w.shape
        return w.reshape(e, halves, f // halves, KH, P).transpose(0, 4, 3, 1, 2)

    def shared_first(w, s):
        return np.concatenate([s[None], w], 0)

    gu0 = np.stack([split(a["L0_ffn_gate_w"], 2), split(a["L0_ffn_up_w"], 2)], 4)
    gu1 = np.stack([split(shared_first(a["L1_ffn_w1"], a["L1_ffn_sw1"]), 1),
                    split(shared_first(a["L1_ffn_w3"], a["L1_ffn_sw3"]), 1)], 4)
    d0 = a["L0_ffn_down_w"].transpose(0, 2, 1)
    d1 = shared_first(a["L1_ffn_w2"], a["L1_ffn_sw2"]).transpose(0, 2, 1)
    cut = (len(KF0) - 1) * P
    arrays = {
        "x": a["x"].reshape(T, H), "small": small, "vecs": vecs, "router": router.transpose(1, 0, 2),
        "const_f": const_f, "const_b": const_b.astype(mybir.dt.np(mybir.dt.bfloat16)),
        "gu0": gu0.reshape(E0, P, GU0),
        "wd0a": d0[:, :cut].reshape(E0, cut // P, P, H).transpose(0, 2, 1, 3).reshape(E0, P, cut // P * H),
        "wd0b": d0[:, cut:],
        "gu1": gu1.reshape(E1 + 1, P, GU1), "wd1a": d1[:, :P], "wd1b": d1[:, P:],
    }
    arrays = {k: np.ascontiguousarray(v) for k, v in arrays.items()}
    nc = bacc.Bacc("TRN2", target_bir_lowering=False, num_devices=1)
    aps = [nc.dram_tensor(k, v.shape, mybir.dt.from_np(v.dtype), kind="ExternalInput").ap() for k, v in arrays.items()]
    out = nc.dram_tensor("out", (T, H), mybir.dt.float32, kind="ExternalOutput").ap()
    build(nc, *aps, out)
    r = run_bass_kernel_spmd(nc, [arrays], core_ids=[0])
    return r.results[0]["out"].reshape(B, N, H)
```

```python
import concourse.bass as bass
from concourse import mybir
from contextlib import ExitStack

P = 128
B, N, H, D = 4, 256, 256, 64
T = B * N
NT = T // P
KH = H // P
E0, F0 = 8, 688
E1, F1 = 15, 176
SHARED = 0


def most_tiles(experts):
    return min(experts * (T // P), (2 * T + (P - 1) * experts) // P)


S0, S1 = most_tiles(E0), most_tiles(E1)
KF0 = [(j, min(P, F0 - j * P)) for j in range(-(-F0 // P))]
KF1 = [(j, min(P, F1 - j * P)) for j in range(-(-F1 // P))]
CH0 = F0 // 2
GU0, GU1 = KH * 2 * F0, KH * 2 * F1
WD0, WD1 = len(KF0) * H, len(KF1) * H
GUALL = E0 * GU0
WDALL = E0 * WD0



def second_weights():
    had_gu = had_dn = 0
    for k in range(1, E0):
        gu, dn = min(E1 + 1, k * GU0 // GU1), min(E1 + 1, k * WD0 // WD1)
        if gu > had_gu or dn > had_dn:
            yield k, had_gu, gu, had_dn, dn
        had_gu, had_dn = gu, dn


C_ID = 0
C_DESC = C_ID + P
C_THR = C_DESC + 16
C_LT = C_THR + NT - 1
C_SLOT = C_LT + E1 * E1
C_NH = C_SLOT + S1
C_VAL = C_NH + 1
C_PAD = C_VAL + 4 * NT
C_ALL = C_PAD + S1
H_TRI, H_ONE, H_LO, H_ALL = 0, P, 2 * P, 3 * P
RING = 4

M_CTX = 0
M_WK = M_CTX + T
M_WJ = M_WK + D
M_WI = M_WJ + P
M_ALL = M_WI + 1
M_ROWS = 80

V_GAMMA, V_BETA, V_GX, V_GF = 0, N, 2 * N, 2 * N + 2
V_ALL = 2 * N + 4

LN_EPS = 1e-5
SIM_EPS = 1e-6
SIM_SCALE = float(N) ** -0.5
NEVER = -3.0e38


def build(nc, x, small, vecs, router, const_f, const_h, gu0, wd0a, wd0b, gu1, wd1a, wd1b, out):
    fp32, fp16, i32 = mybir.dt.float32, mybir.dt.float16, mybir.dt.int32
    ALU = mybir.AluOpType
    ACT = mybir.ActivationFunctionType
    X = mybir.AxisListType.X

    rows = nc.dram_tensor("rows", (T, H), fp32).ap()
    results = nc.dram_tensor("results", (2 * T + S1 * P, H), fp32).ap()
    rows_t = rows.rearrange("(i p) h -> p i h", p=P)
    results_t = results[0:2 * T, :].rearrange("(i p k) h -> p i (k h)", p=P, k=2)
    x_t = x.rearrange("(i p) h -> p i h", p=P)
    out_t = out.rearrange("(i p) h -> p i h", p=P)

    ctx = ExitStack()
    with ctx:
        def sb(name, shape, dt=fp32):
            return ctx.enter_context(nc.sbuf_tensor(name, shape, dt))

        def sem(name):
            return ctx.enter_context(nc.semaphore(name))

        wgu = sb("wgu", [P, GUALL])
        wdn = sb("wdn", [P, WDALL])
        xs = sb("xs", [P, NT, H])
        xn = sb("xn", [P, NT, H])
        edge = sb("edge", [P, NT, H])
        small_sb = sb("small_sb", [M_ROWS, M_ALL])
        vec_sb = sb("vec_sb", [P, V_ALL])
        router_sb = sb("router_sb", [P, KH, E0 + E1])
        cf = sb("cf", [P, C_ALL])
        ch = sb("ch", [P, H_ALL], fp16)
        gamma16 = sb("gamma16", [P, N])
        tg = sb("tg", [P, 4])
        edge_c = sb("edge_c", [P, 2])
        lower = sb("lower", [P, 2 * T])
        kvT = lower[0:D, 0:T]
        kv = sb("kv", [P, NT, D])
        half_si = sb("half_si", [P, NT])
        half_b = sb("half_b", [P, NT])
        pT = sb("pT", [P, 2, H])
        oT = lower[0:D, T:2 * T].rearrange("p (i n) -> p i n", n=P)
        z = sb("z", [P, 4, N])
        e = sb("e", [P, 2, N])
        st = sb("st", [P, NT, 6])
        mv = sb("mv", [P, NT, 2])
        ve = sb("ve", [P, NT])
        rs = sb("rs", [P, NT])
        mx = sb("mx", [P, NT])
        nmx = sb("nmx", [P, NT])
        sm = sb("sm", [P, NT])
        rc = sb("rc", [P, NT])
        cc = sb("cc", [P, NT])
        x_in = sb("x_in", [P, RING, H])
        xT = sb("xT", [P, 2, H])
        th = sb("th", [P, F0])
        hh = sb("hh", [P, F0])
        hT = sb("hT", [P, len(KF0) * P])
        y_sb = sb("y_sb", [P, RING, H])
        lo1 = z[:].bitcast(fp16).rearrange("p a b -> p (a b)").rearrange("p (i n) -> p i n", n=P)
        hi1 = pT[:].bitcast(fp16).rearrange("p a b -> p (a b)")[:, 0:2 * NT * S1].rearrange("p (i s) -> p i s", s=S1)
        hi2 = e[:].bitcast(fp16).rearrange("p a b -> p (a b)")[:, 0:4 * NT * S1].rearrange(
            "p (i q s) -> p i q s", q=2, s=S1)
        val16 = sb("val16", [P, 2 * NT, 2], fp16)
        free = (E1 + 1) * GU1
        y_got = wgu[:, free:free + 2 * NT * H].rearrange("p (i k h) -> p i k h", k=2, h=H)
        xnT = wgu[:, free + 2 * NT * H:free + 3 * NT * H].rearrange("p (i h) -> p i h", h=H)

        psum = [ctx.enter_context(nc.psum_tensor(f"bank{i}", [P, 512], fp32)) for i in range(8)]
        ident = cf[:, C_ID:C_ID + P]

        x_here = [sem(f"x_here{i}") for i in range(B)]
        small_here, vec_here, router_here = sem("small_here"), sem("vec_here"), sem("router_here")
        const_here, constb_here = sem("const_here"), sem("constb_here")
        w0_here = [sem(f"w0_here{i}") for i in range(E0)]
        w1_here = [sem(f"w1_here{i}") for i, _ in enumerate(second_weights())]
        out_stored = sem("out_stored")
        kvT_done, kv_done, kvT_copied, kv_copied = sem("kvT_done"), sem("kv_done"), sem("kvT_copied"), sem("kv_copied")
        gates_done = sem("gates_done")
        p_var, p_rstd, p_ready = sem("p_var"), sem("p_rstd"), sem("p_ready")
        pT_done, pT_copied = sem("pT_done"), sem("pT_copied")
        oT_done, oT_copied, sim_done = sem("oT_done"), sem("oT_copied"), sem("sim_done")
        s_var, s_rstd, s_read, z_scaled = sem("s_var"), sem("s_rstd"), sem("s_read"), sem("z_scaled")
        gamma_ready, z_ready, exp_done = sem("gamma_ready"), sem("z_ready"), sem("exp_done")
        dve_step = sem("dve_step")
        pool_step = sem("pool_step")
        x2_var, x2_rstd = sem("x2_var"), sem("x2_rstd")
        edge_added = sem("edge_added")
        sj_done, si_done, si_copied, edge_th, edge_c_ready, edge_ready = (
            sem("sj_done"), sem("si_done"), sem("si_copied"), sem("edge_th"), sem("edge_c_ready"), sem("edge_ready"))

        kept, filled = {}, [0]
        LARGEST = {"oh": 2 * NT * E1, "w12": 2 * NT * E1, "A": (NT + 1) * E1, "cmp": E1 * (NT - 1),
                   "lt": E1 * E1, "scmp": S1 * (E1 - 1), "place": 2 * NT, "lo": 2 * NT, "hi": 2 * NT, "lof": 2 * NT, "L": NT * E1, "L2": NT * E1, "w": NT * E1, "R2": NT * E1}
        STAY = ("c1", "c2", "tok", "dst", "owner")

        def work(name, *shape, dt=fp32):
            if name not in kept:
                most = LARGEST.get(name, S1)
                if name == "scmp":
                    kept[name] = lower[:, 0:most]
                elif name in STAY:
                    kept[name] = sb("route_" + name, [P, most], dt)
                else:
                    flat = lower[:, filled[0]:filled[0] + most]
                    filled[0] += most
                    kept[name] = flat if dt == fp32 else flat.bitcast(dt)
            size = 1
            for x in shape:
                size *= x
            flat = kept[name][:, 0:size]
            if len(shape) == 1:
                return flat
            if len(shape) == 2:
                return flat.rearrange("p (a b) -> p a b", b=shape[1])
            return flat.rearrange("p (a b c) -> p a b c", b=shape[1], c=shape[2])

        class Mixture:

            def __init__(m, n, experts, tiles, kf, chunk, ahead):
                m.split = 4 if n == 0 else 1
                m.n, m.E, m.S, m.kf, m.ahead = n, experts, tiles, kf, ahead
                m.logits = psum[6][:, H:H + NT * experts].rearrange("p (i e) -> p i e", e=experts)
                m.ranks = psum[6][:, 512 - (NT + 1) * experts:512].rearrange("p (i e) -> p i e", e=experts)
                m.inverse = psum[3][:, 0:2 * tiles].rearrange("p (q s) -> p q s", q=2)
                m.var, m.rstd, m.xn_ready = sem(f"var{n}"), sem(f"rstd{n}"), sem(f"xn_ready{n}")
                m.xnT_done, m.xnT_copied = sem(f"xnT_done{n}"), sem(f"xnT_copied{n}")
                m.logits_done, m.picked = sem(f"logits_done{n}"), sem(f"picked{n}")
                m.shifted, m.exps = sem(f"shifted{n}"), sem(f"exps{n}")
                m.ranks_done = sem(f"ranks_done{n}")
                m.onehots_ready, m.inverse_done = sem(f"onehots_ready{n}"), sem(f"inverse_done{n}")
                m.lists_ready, m.experts_ready = sem(f"lists_ready{n}"), sem(f"experts_ready{n}")
                m.rows_stored = sem(f"rows_stored{n}")
                m.x_loaded = [sem(f"x_loaded{n}{r}") for r in range(RING)]
                m.xT_done, m.xT_copied = sem(f"xT_done{n}"), sem(f"xT_copied{n}")
                m.gu_done, m.th_done, m.h_made = sem(f"gu_done{n}"), sem(f"th_done{n}"), sem(f"h_made{n}")
                m.hT_done = sem(f"hT_done{n}")
                m.hT_copied_a, m.hT_copied_v = sem(f"hT_copied_a{n}"), sem(f"hT_copied_v{n}")
                m.y_done, m.y_copied = sem(f"y_done{n}"), sem(f"y_copied{n}")
                m.y_stored = [sem(f"y_stored{n}{r}") for r in range(RING)]
                m.y_here = [sem(f"y_here{n}{b}") for b in range(B)]
                m.x_new = sem(f"x_new{n}")
                m.half, m.z_added = sem(f"half{n}"), sem(f"z_added{n}")
                m.L = sb(f"L{n}", [P, NT, experts])
                m.w = sb(f"w{n}", [P, NT, experts])
                W, k2 = experts, 2 * NT
                m.oh, m.w12 = work("oh", 2, NT, W), work("w12", 2, NT, W)
                m.L, m.L2, m.w, m.R2 = (work(x, NT, W) for x in ("L", "L2", "w", "R2"))
                m.A = work("A", NT + 1, W, dt=fp16)
                m.place, m.lo, m.hi = (work(x, k2, dt=i32) for x in ("place", "lo", "hi"))
                m.lof = work("lof", k2)
                m.tok, m.dst, m.pad = work("tok", tiles, dt=i32), work("dst", tiles, dt=i32), work("pad", tiles)
                m.v1, m.v2, m.m, m.d, m.ed = (work(x, NT) for x in ("v1", "v2", "m", "d", "ed"))
                m.den, m.p1, m.c1, m.c2 = (work(x, NT) for x in ("den", "p1", "c1", "c2"))
                m.cmp, m.lt = work("cmp", W, NT - 1), work("lt", W, W)
                m.tl, m.base, m.incl = work("tl", W), work("base", W), work("incl", W)
                m.scmp, m.ownf = work("scmp", tiles, W - 1), work("ownf", tiles)
                m.owner = work("owner", tiles, dt=i32)

        mix = [Mixture(0, E0, S0, KF0, CH0, 1), Mixture(1, E1, S1, KF1, F1, 2)]

        def steps(eng, step, total, full):
            for s in range(RING):
                step(s, s)
            groups = full // RING
            with eng.Fori(1, groups) as j:
                for r in range(RING):
                    step(j * RING + r, r)
            for s in range(RING * groups, total):
                step(s, s % RING)

        def landed(n, r):
            return n * (16 // RING) + (16 - 16 // RING * r)

        def since(eng, semaphore, value):
            if not isinstance(value, int) or value > 0:
                eng.wait_ge(semaphore, value)

        def below(s, limit):
            return not isinstance(s, int) or s < limit

        SCORES = (3, 4, 5, 7)

        block = ctx.enter_context(nc.Block())

        @block.sync
        def _(sp):
            for b in range(B):
                sp.dma_start(xs[:, 2 * b:2 * b + 2, :], x_t[:, 2 * b:2 * b + 2, :]).then_inc(x_here[b], 16)
            sp.dma_start(router_sb[:], router).then_inc(router_here, 16)
            sp.dma_start(ch[:], const_h).then_inc(constb_here, 16)
            for n in range(E0):
                sp.dma_start(wgu[:, n * GU0:(n + 1) * GU0], gu0[n]).then_inc(w0_here[n], 16)
                tail = KF0[-1][0] * H
                sp.dma_start(wdn[:, n * WD0:n * WD0 + tail], wd0a[n]).then_inc(w0_here[n], 16)
                sp.dma_start(wdn[0:KF0[-1][1], n * WD0 + tail:(n + 1) * WD0], wd0b[n]).then_inc(w0_here[n], 16)
            for m in mix:
                for b in range(B):
                    sp.wait_ge(m.xn_ready, 2 * b + 2)
                    sp.dma_start(rows_t[:, 2 * b:2 * b + 2, :], xn[:, 2 * b:2 * b + 2, :]).then_inc(m.rows_stored, 16)
                if m is mix[0]:
                    for n, (k, gu_a, gu_z, dn_a, dn_z) in enumerate(second_weights()):
                        sp.wait_ge(mix[0].y_done, most_tiles(k))
                        if gu_z > gu_a:
                            sp.dma_start(
                                wgu[:, gu_a * GU1:gu_z * GU1].rearrange("p (e n) -> p e n", n=GU1),
                                gu1[gu_a:gu_z].rearrange("e p n -> p e n")).then_inc(w1_here[n], 16)
                        if dn_z > dn_a:
                            dn = wdn[:, dn_a * WD1:dn_z * WD1].rearrange("p (e n) -> p e n", n=WD1)
                            sp.dma_start(dn[:, :, 0:H], wd1a[dn_a:dn_z].rearrange("e p n -> p e n")
                                                ).then_inc(w1_here[n], 16)
                            sp.dma_start(dn[0:KF1[1][1], :, H:2 * H], wd1b[dn_a:dn_z].rearrange("e p n -> p e n")
                                                ).then_inc(w1_here[n], 16)
                for r in range(RING):
                    last = (m.S - 1 - r) // RING * RING + r
                    sp.wait_ge(m.y_stored[r], landed(last, r))
                for b in range(B):
                    sp.dma_start(y_got[:, 2 * b:2 * b + 2, :, :].rearrange("p i k h -> p i (k h)"),
                                 results_t[:, 2 * b:2 * b + 2, :]).then_inc(m.y_here[b], 16)
            for i in range(NT):
                sp.wait_ge(mix[1].x_new, i + 1)
                sp.dma_start(out_t[:, i, :], xs[:, i, :]).then_inc(out_stored, 16)
            sp.wait_ge(out_stored, 16 * NT)

        @block.gpsimd
        def _(pool):
            minus_half = cf[:, C_NH:C_NH + 1].to_broadcast([P, 2])
            pool.wait_ge(const_here, 16)

            def rstd(b, var, ready):
                pool.wait_ge(var, b + 1)
                nc.gpsimd.tensor_tensor(rs[:, 2 * b:2 * b + 2], ve[:, 2 * b:2 * b + 2], minus_half,
                                        ALU.pow).then_inc(ready, 1)

            def scale_z(i):
                pool.wait_ge(s_read, i + 1)
                nc.gpsimd.tensor_tensor(z[:, i % 4, :], z[:, i % 4, :], gamma16[:], ALU.mult).then_inc(z_scaled, 1)

            for b in range(B):
                rstd(b, p_var, p_rstd)
            rstd(0, s_var, s_rstd)
            pool.wait_ge(gamma_ready, 1)
            for b in range(B):
                scale_z(2 * b)
                scale_z(2 * b + 1)
                if b >= 1:
                    rstd(b - 1, mix[0].var, mix[0].rstd)
                if b + 1 < B:
                    rstd(b + 1, s_var, s_rstd)
            rstd(B - 1, mix[0].var, mix[0].rstd)

            def gather(m, t):
                nc.gpsimd.indirect_dma_start(
                    out=x_in[:, t % RING, :], out_offset=None, in_=rows,
                    in_offset=bass.IndirectOffsetOnAxis(ap=m.tok[:, t:t + 1], axis=0)).then_inc(m.x_loaded[t % RING], 16)

            def scatter(m, s):
                nc.gpsimd.indirect_dma_start(
                    out=results, out_offset=bass.IndirectOffsetOnAxis(ap=m.dst[:, s:s + 1], axis=0),
                    in_=y_sb[:, s % RING, :], in_offset=None).then_inc(m.y_stored[s % RING], 16)

            def exchange(m, extra):
                pool.wait_ge(m.lists_ready, 1)
                pool.wait_ge(m.rows_stored, 16 * B)
                lead = m.ahead + 1 + RING
                for t in range(lead):
                    since(pool, m.xT_done, t - RING + 1)
                    gather(m, t)
                for s in range(m.S):
                    if s + lead < m.S:
                        pool.wait_ge(m.xT_done, s + lead - RING + 1)
                        gather(m, s + lead)
                    pool.wait_ge(m.y_copied, s + 1)
                    scatter(m, s)
                    extra(s)

            pool.wait_ge(edge_c_ready, 1)

            def finish_edge(s):
                if s < RING:
                    for i in range(2 * s, 2 * s + 2):
                        pool.wait_ge(edge_th, i + 1)
                        nc.gpsimd.tensor_scalar(edge[:, i, :], edge[:, i, :], edge_c[:, 0:1], edge_c[:, 0:1],
                                                ALU.mult, ALU.add).then_inc(edge_ready, 1)

            exchange(mix[0], finish_edge)
            for b in range(B):
                rstd(b, x2_var, x2_rstd)
                for i in (2 * b, 2 * b + 1):
                    pool.wait_ge(mix[0].x_new, i + 1)
                    nc.gpsimd.tensor_tensor(edge[:, i, :], edge[:, i, :], xs[:, i, :], ALU.add).then_inc(edge_added, 1)
                rstd(b, mix[1].var, mix[1].rstd)
            exchange(mix[1], lambda s: None)

        @block.scalar
        def _(act):
            act.dma_start(cf[:], const_f).then_inc(const_here, 16)
            act.dma_start(small_sb[:], small).then_inc(small_here, 16)
            act.dma_start(vec_sb[:], vecs.to_broadcast([P, V_ALL])).then_inc(vec_here, 16)
            act.wait_ge(vec_here, 16)
            nc.scalar.activation(tg[:], vec_sb[:, V_GX:V_GX + 4], ACT.Tanh).then_inc(gates_done, 1)
            for h in range(2):
                act.wait_ge(kvT_done, h + 1)
                nc.scalar.activation(kvT[:, h * 512:(h + 1) * 512], psum[3 + h][0:D, :], ACT.Copy).then_inc(kvT_copied, 1)
            act.wait_ge(kv_done, 1)
            nc.scalar.activation(kv[:].rearrange("p i d -> p (i d)"), psum[5][:, :], ACT.Copy).then_inc(kv_copied, 1)

            def copy_pT(i):
                act.wait_ge(pT_done, i + 1)
                since(act, oT_done, i - 1)
                nc.scalar.activation(pT[:, i % 2, :], psum[i % 2][:, 0:H], ACT.Copy).then_inc(pT_copied, 1)

            def copy_oT(i):
                act.wait_ge(oT_done, i + 1)
                nc.scalar.activation(oT[:, i, :], psum[2][0:D, 0:P], ACT.Copy).then_inc(oT_copied, 1)

            def exps(b):
                for i in (2 * b, 2 * b + 1):
                    act.wait_ge(z_ready, b + 1)
                    nc.scalar.activation(e[:, i % 2, :], z[:, i % 4, :], ACT.Exp, bias=nmx[:, i:i + 1],
                                         accum_out=sm[:, i:i + 1]).then_inc(exp_done, 1)

            def copy_xnT(m, i, dst):
                act.wait_ge(m.xnT_done, i + 1)
                nc.scalar.activation(dst, psum[6][:, 0:H], ACT.Copy).then_inc(m.xnT_copied, 1)

            copy_pT(0)
            for i in range(NT):
                if i + 1 < NT:
                    copy_pT(i + 1)
                copy_oT(i)
                if i == 5:
                    exps(0)
            for b in range(1, B):
                exps(b)
                for i in (2 * b - 2, 2 * b - 1):
                    copy_xnT(mix[0], i, xT[:, i % 2, :])
            for i in (NT - 2, NT - 1):
                copy_xnT(mix[0], i, xT[:, i % 2, :])

            def route_exps(m):
                act.wait_ge(m.shifted, 1)
                nc.scalar.activation(m.ed, m.d, ACT.Exp).then_inc(m.exps, 1)
                if m.n == 1:
                    nc.scalar.activation(m.L2.rearrange("p i e -> p (i e)"),
                                         m.L2.rearrange("p i e -> p (i e)"), ACT.Exp).then_inc(m.exps, 1)

            route_exps(mix[0])
            act.wait_ge(si_done, 1)
            nc.scalar.activation(half_si[:], psum[2][:, 0:NT], ACT.Copy, scale=0.5).then_inc(si_copied, 1)
            act.wait_ge(si_copied, 1)
            act.wait_ge(sj_done, 2)
            for i in range(NT):
                b = i // 2
                nc.scalar.activation(edge[:, i, :], psum[4 + b // 2][:, (b % 2) * N:(b % 2 + 1) * N], ACT.Tanh,
                                     bias=half_si[:, i:i + 1], scale=0.5).then_inc(edge_th, 1)

            def tanh_half(m, t, r):
                if m.n == 0:
                    for c in range(2):
                        act.wait_ge(m.gu_done, 2 * t + c + 1)
                        since(act, m.h_made, 2 * (t - 1) + c + 1)
                        nc.scalar.activation(th[:, c * CH0:(c + 1) * CH0], psum[2 * c][:, 0:CH0], ACT.Tanh,
                                             scale=0.5).then_inc(m.th_done, 1)
                else:
                    act.wait_ge(m.gu_done, t + 1)
                    since(act, m.h_made, t - 1)
                    nc.scalar.activation(th[:, r * F1:(r + 1) * F1], psum[r][:, 0:F1], ACT.Tanh,
                                         scale=0.5).then_inc(m.th_done, 1)

            def copy_hT(m, s, r):
                act.wait_ge(m.hT_done, s + 1)
                n = 512 if m.n == 0 else P
                nc.scalar.activation(hT[:, 0:n], psum[4][:, 0:n], ACT.Copy, scale=0.5).then_inc(m.hT_copied_a, 1)

            m = mix[0]
            tanh_half(m, 0, 0)

            def step0(s, r):
                copy_hT(m, s, r)
                if below(s, m.S - 1):
                    tanh_half(m, s + 1, (r + 1) % 2)
                act.wait_ge(m.y_done, s + 1)
                if not isinstance(s, int) or s >= RING:
                    act.wait_ge(m.y_stored[r], s * 4 - 4 * r)
                nc.scalar.activation(y_sb[:, r, :], psum[7][:, 0:H], ACT.Copy).then_inc(m.y_copied, 1)

            steps(act, step0, m.S, m.S - 1)

            m1 = mix[1]
            for i in range(NT):
                copy_xnT(m1, i, xnT[:, i, :])
            route_exps(m1)
            tanh_half(m1, 0, 0)
            tanh_half(m1, 1, 1)
            for i in range(NT):
                copy_hT(m1, i, i % 2)
                tanh_half(m1, i + 2, i % 2)

            def step1(s, r):
                copy_hT(m1, s + NT, r)
                if below(s, m1.S - 2):
                    tanh_half(m1, s + (NT + 2), r % 2)
                act.wait_ge(m1.y_done, s + (NT + 1))
                if not isinstance(s, int) or s >= RING:
                    act.wait_ge(m1.y_stored[r], s * 4 - 4 * r)
                nc.scalar.activation(y_sb[:, r, :], psum[7][:, 0:H], ACT.Copy).then_inc(m1.y_copied, 1)

            steps(act, step1, m1.S, m1.S - 2)

        @block.vector
        def _(dve):
            count = [0]

            def then(instruction):
                count[0] += 1
                instruction.then_inc(dve_step, 1)
                dve.wait_ge(dve_step, count[0])

            def did(instruction):
                count[0] += 1
                instruction.then_inc(dve_step, 1)
                return count[0]

            def after(n):
                dve.wait_ge(dve_step, n)

            def stats(src, b, eps, scale, signal):
                tiles = (2 * b, 2 * b + 1)
                ends = [did(nc.vector.bn_stats(st[:, i, :], src(i))) for i in tiles]
                for i, end in zip(tiles, ends):
                    after(end)
                    last = did(nc.vector.bn_aggr(mv[:, i, :], st[:, i, :]))
                after(last)
                nc.vector.tensor_scalar(ve[:, 2 * b:2 * b + 2], mv[:, 2 * b:2 * b + 2, 1], scale, eps,
                                        ALU.mult, ALU.add).then_inc(signal, 1)

            def rows_of_x(i):
                return xs[:, i, :]

            def x_norm(b, rstd, signal):
                dve.wait_ge(rstd, b + 1)
                for i in (2 * b, 2 * b + 1):
                    nc.vector.tensor_scalar(xn[:, i, :], xs[:, i, :], mv[:, i, 0:1], rs[:, i:i + 1],
                                            ALU.subtract, ALU.mult).then_inc(signal, 1)

            for b in range(B + 1):
                if b < B:
                    dve.wait_ge(x_here[b], 16)
                    stats(rows_of_x, b, LN_EPS, 1.0, p_var)
                if b >= 1:
                    x_norm(b - 1, p_rstd, p_ready)
            dve.wait_ge(vec_here, 16)
            dve.wait_ge(gates_done, 1)
            nc.vector.tensor_scalar(gamma16[:], vec_sb[:, V_GAMMA:V_GAMMA + N], SIM_SCALE, None,
                                    ALU.mult).then_inc(gamma_ready, 1)
            nc.vector.tensor_scalar(edge_c[:, 0:1], tg[:, 1:2], 0.3, None, ALU.mult).then_inc(edge_c_ready, 1)
            nc.vector.tensor_scalar(edge_c[:, 1:2], tg[:, 1:2], 0.4, None, ALU.mult)
            nc.vector.tensor_copy(val16[:].rearrange("p i q -> p (i q)"), cf[:, C_VAL:C_VAL + 4 * NT])

            def score_bank(i):
                return psum[SCORES[i % 4]][:, 0:N]

            def score_stats(b):
                dve.wait_ge(sim_done, 2 * b + 2)
                stats(score_bank, b, SIM_EPS, SIM_SCALE * SIM_SCALE, s_var)

            def score_norm(b):
                dve.wait_ge(s_rstd, b + 1)
                for i in (2 * b, 2 * b + 1):
                    nc.vector.tensor_scalar(z[:, i % 4, :], score_bank(i), mv[:, i, 0:1], rs[:, i:i + 1],
                                            ALU.subtract, ALU.mult).then_inc(s_read, 1)

            def score_shift(b):
                for i in (2 * b, 2 * b + 1):
                    dve.wait_ge(z_scaled, i + 1)
                    last = did(nc.vector.tensor_tensor_reduce(
                        out=z[:, i % 4, :], in0=z[:, i % 4, :], in1=vec_sb[:, V_BETA:V_BETA + N], scale=1.0,
                        scalar=NEVER, op0=ALU.add, op1=ALU.max, accum_out=mx[:, i:i + 1]))
                after(last)
                nc.vector.tensor_scalar(nmx[:, 2 * b:2 * b + 2], mx[:, 2 * b:2 * b + 2], -1.0, None,
                                        ALU.mult).then_inc(z_ready, 1)

            def attend(b):
                dve.wait_ge(exp_done, 2 * b + 2)
                then(nc.vector.reciprocal(rc[:, 2 * b:2 * b + 2], sm[:, 2 * b:2 * b + 2]))
                then(nc.vector.tensor_scalar(cc[:, 2 * b:2 * b + 2], rc[:, 2 * b:2 * b + 2], tg[:, 0:1], None,
                                             ALU.mult))
                for i in (2 * b, 2 * b + 1):
                    last = did(nc.vector.scalar_tensor_tensor(
                        out=xs[:, i, :], in0=e[:, i % 2, :], scalar=cc[:, i:i + 1], in1=xs[:, i, :],
                        op0=ALU.mult, op1=ALU.add))
                after(last)
                stats(rows_of_x, b, LN_EPS, 1.0, mix[0].var)

            score_stats(0)
            for b in range(B):
                score_norm(b)
                if b >= 1:
                    attend(b - 1)
                if b + 1 < B:
                    score_stats(b + 1)
                score_shift(b)
                if b >= 1:
                    x_norm(b - 1, mix[0].rstd, mix[0].xn_ready)
            attend(B - 1)
            x_norm(B - 1, mix[0].rstd, mix[0].xn_ready)

            def route(m):
                E = m.E
                desc = cf[:, C_DESC:C_DESC + E].unsqueeze(1).to_broadcast([P, NT, E])
                lt = cf[:, C_LT:C_LT + E1 * E1].rearrange("p (a b) -> p a b", a=E1)[:, 0:E, 0:E]

                def wide(v):
                    return v.unsqueeze(2).to_broadcast([P, NT, E])

                def first_best(logits, best, onehot):
                    then(nc.vector.tensor_reduce(out=best, in_=logits, axis=X, op=ALU.max))
                    then(nc.vector.tensor_tensor(m.w, logits, wide(best), ALU.is_equal))
                    then(nc.vector.tensor_tensor(m.w, m.w, desc, ALU.mult))
                    then(nc.vector.tensor_reduce(out=m.m, in_=m.w, axis=X, op=ALU.max))
                    then(nc.vector.tensor_tensor(onehot, m.w, wide(m.m), ALU.is_equal))

                dve.wait_ge(m.logits_done, NT)
                then(nc.vector.tensor_copy(m.L, m.logits))
                first_best(m.L, m.v1, m.oh[:, 0])
                then(nc.vector.scalar_tensor_tensor(out=m.L2, in0=m.oh[:, 0], scalar=NEVER, in1=m.L,
                                                    op0=ALU.mult, op1=ALU.add))
                first_best(m.L2, m.v2, m.oh[:, 1])
                nc.vector.memset(m.A[:, NT, :], 0.0)
                nc.vector.tensor_tensor(m.A[:, 0:NT, :], m.oh[:, 0], m.oh[:, 1], ALU.add).then_inc(m.picked, 1)
                if m.n == 1:
                    nc.vector.tensor_tensor(m.L2, m.L, wide(m.v1), ALU.subtract)
                nc.vector.tensor_tensor(m.d, m.v2, m.v1, ALU.subtract).then_inc(m.shifted, 1)

                dve.wait_ge(m.ranks_done, 1)
                then(nc.vector.tensor_tensor(
                    m.cmp, m.ranks[:, NT, :].unsqueeze(2).to_broadcast([P, E, NT - 1]),
                    cf[:, C_THR:C_THR + NT - 1].unsqueeze(1).to_broadcast([P, E, NT - 1]), ALU.is_gt))
                then(nc.vector.tensor_reduce(out=m.tl, in_=m.cmp, axis=X, op=ALU.add))
                then(nc.vector.tensor_scalar(m.tl, m.tl, 1.0, None, ALU.add))
                then(nc.vector.tensor_tensor(m.lt, lt, m.tl.unsqueeze(1).to_broadcast([P, E, E]), ALU.mult))
                then(nc.vector.tensor_reduce(out=m.base, in_=m.lt, axis=X, op=ALU.add))
                then(nc.vector.scalar_tensor_tensor(
                    out=m.R2, in0=m.base.unsqueeze(1).to_broadcast([P, NT, E]), scalar=float(P),
                    in1=m.ranks[:, 0:NT, :], op0=ALU.mult, op1=ALU.add))
                then(nc.vector.tensor_tensor(m.w12, m.oh,
                                             m.R2.unsqueeze(1).to_broadcast([P, 2, NT, E]), ALU.mult))
                then(nc.vector.tensor_reduce(out=m.lof, in_=m.w12.rearrange("p k i e -> p (k i) e"),
                                             axis=X, op=ALU.add))
                then(nc.vector.tensor_copy(m.place, m.lof))
                nc.vector.tensor_scalar(m.lo, m.place, P - 1, None, ALU.bitwise_and)
                then(nc.vector.tensor_scalar(m.hi, m.place, 7, None, ALU.logical_shift_right))
                nc.vector.tensor_copy(m.lof, m.lo)
                then(nc.vector.tensor_tensor(
                    hi1[:, :, 0:m.S], cf[:, C_SLOT:C_SLOT + m.S].unsqueeze(1).to_broadcast([P, 2 * NT, m.S]),
                    m.hi.unsqueeze(2).to_broadcast([P, 2 * NT, m.S]), ALU.is_equal))
                for q in range(2):
                    nc.vector.tensor_tensor(
                        hi2[:, :, q, 0:m.S], hi1[:, :, 0:m.S],
                        val16[:, :, q:q + 1].to_broadcast([P, 2 * NT, m.S]), ALU.mult)
                for i in range(2 * NT):
                    nc.vector.tensor_scalar(lo1[:, i, :], ch[:, H_LO:H_LO + P], m.lof[:, i:i + 1], None,
                                            ALU.is_equal).then_inc(m.onehots_ready, 1)
                then(nc.vector.tensor_tensor(m.incl, m.base, m.tl, ALU.add))
                then(nc.vector.tensor_tensor(
                    m.scmp[0:1], cf[0:1, C_SLOT:C_SLOT + m.S].unsqueeze(2).to_broadcast([1, m.S, E - 1]),
                    m.incl[0:1, 0:E - 1].unsqueeze(1).to_broadcast([1, m.S, E - 1]), ALU.is_ge))
                then(nc.vector.tensor_reduce(out=m.ownf[0:1, :], in_=m.scmp[0:1], axis=X, op=ALU.add))
                nc.vector.tensor_copy(m.owner[0:1, :], m.ownf[0:1, :]).then_inc(m.experts_ready, 1)
                dve.wait_ge(m.inverse_done, 1)
                nc.vector.tensor_copy(m.tok, m.inverse[:, 0, :])
                then(nc.vector.scalar_tensor_tensor(out=m.pad, in0=m.inverse[:, 1, :], scalar=0.0,
                                                    in1=cf[:, C_PAD:C_PAD + m.S], op0=ALU.is_equal, op1=ALU.mult))
                nc.vector.scalar_tensor_tensor(out=m.dst, in0=m.inverse[:, 1, :], scalar=-1.0, in1=m.pad,
                                               op0=ALU.add, op1=ALU.add).then_inc(m.lists_ready, 1)
                dve.wait_ge(m.exps, m.n + 1)
                if m.n == 0:
                    then(nc.vector.tensor_scalar(m.den, m.ed, 1.0, None, ALU.add))
                else:
                    then(nc.vector.tensor_reduce(out=m.den, in_=m.L2, axis=X, op=ALU.add))
                then(nc.vector.reciprocal(m.p1, m.den))
                then(nc.vector.tensor_scalar(m.c1, m.p1, tg[:, 2 + m.n:3 + m.n], None, ALU.mult))
                then(nc.vector.tensor_tensor(m.c2, m.c1, m.ed, ALU.mult))

            route(mix[0])

            def copy_hT(m, s, r):
                dve.wait_ge(m.hT_done, s + 1)
                if m.n == 0:
                    nc.vector.tensor_scalar(hT[:, 512:640], psum[5][:, 0:P], 0.5, None, ALU.mult)
                    nc.vector.tensor_scalar(hT[0:KF0[-1][1], 640:768], psum[5][0:KF0[-1][1], P:2 * P], 0.5, None,
                                            ALU.mult).then_inc(m.hT_copied_v, 1)
                else:
                    nc.vector.tensor_scalar(hT[0:KF1[-1][1], P:2 * P], psum[5][0:KF1[-1][1], 0:P], 0.5, None,
                                            ALU.mult).then_inc(m.hT_copied_v, 1)

            def hidden(m, t, r, half_step, halves=(0, 1)):
                if m.n == 0:
                    for c in halves:
                        cols = slice(c * CH0, (c + 1) * CH0)
                        dve.wait_ge(m.th_done, 2 * t + c + 1)
                        nc.vector.scalar_tensor_tensor(out=hh[:, cols], in0=th[:, cols], scalar=1.0,
                                                       in1=psum[2 * c][:, 0:CH0], op0=ALU.add,
                                                       op1=ALU.mult).then_inc(half_step, 1)
                        dve.wait_ge(half_step, 2 * t + c + 1)
                        nc.vector.tensor_tensor(hh[:, cols], hh[:, cols], psum[2 * c + 1][:, 0:CH0],
                                                ALU.mult).then_inc(m.h_made, 1)
                else:
                    cols = slice(r * F1, (r + 1) * F1)
                    dve.wait_ge(m.th_done, t + 1)
                    since(dve, m.hT_done, t - 1)
                    nc.vector.scalar_tensor_tensor(out=hh[:, cols], in0=th[:, cols], scalar=1.0,
                                                   in1=psum[r][:, 0:F1], op0=ALU.add,
                                                   op1=ALU.mult).then_inc(half_step, 1)
                    dve.wait_ge(half_step, t + 1)
                    nc.vector.tensor_tensor(hh[:, cols], hh[:, cols], psum[r][:, F1:2 * F1],
                                            ALU.mult).then_inc(m.h_made, 1)

            def copy_xT(m, t, r):
                dve.wait_ge(m.xT_done, t + 1)
                nc.vector.tensor_copy(xT[:, r, :], psum[6][:, 0:H]).then_inc(m.xT_copied, 1)

            m = mix[0]
            copy_xT(m, 0, 0)
            hidden(m, 0, 0, m.half)
            copy_xT(m, 1, 1)

            def step0(s, r):
                copy_hT(m, s, r)
                if below(s, m.S - 1):
                    hidden(m, s + 1, r, m.half, (0,))
                if below(s, m.S - 2):
                    copy_xT(m, s + 2, r % 2)
                if below(s, m.S - 1):
                    hidden(m, s + 1, r, m.half, (1,))

            steps(dve, step0, m.S, m.S - 2)

            def combine(m, b):
                dve.wait_ge(m.y_here[b], 16)
                ends = [did(nc.vector.scalar_tensor_tensor(
                    out=xs[:, i, :], in0=y_got[:, i, 0, :], scalar=m.c1[:, i:i + 1], in1=xs[:, i, :],
                    op0=ALU.mult, op1=ALU.add)) for i in (2 * b, 2 * b + 1)]
                for i, end in zip((2 * b, 2 * b + 1), ends):
                    after(end)
                    nc.vector.scalar_tensor_tensor(
                        out=xs[:, i, :], in0=y_got[:, i, 1, :], scalar=m.c2[:, i:i + 1], in1=xs[:, i, :],
                        op0=ALU.mult, op1=ALU.add).then_inc(m.x_new, 1)

            m1 = mix[1]

            def second(b):
                combine(mix[0], b)
                dve.wait_ge(mix[0].x_new, 2 * b + 2)
                stats(rows_of_x, b, LN_EPS, 1.0, x2_var)

            def third(b):
                tiles = (2 * b, 2 * b + 1)
                dve.wait_ge(x2_rstd, b + 1)
                then(nc.vector.tensor_scalar(cc[:, 2 * b:2 * b + 2], rs[:, 2 * b:2 * b + 2], edge_c[:, 1:2], None,
                                             ALU.mult))
                ends = [did(nc.vector.tensor_scalar(xn[:, i, :], xs[:, i, :], mv[:, i, 0:1], cc[:, i:i + 1],
                                                    ALU.subtract, ALU.mult)) for i in tiles]
                for i, end in zip(tiles, ends):
                    dve.wait_ge(edge_added, i + 1)
                    after(end)
                    last = did(nc.vector.tensor_tensor(xs[:, i, :], edge[:, i, :], xn[:, i, :], ALU.add))
                after(last)
                stats(rows_of_x, b, LN_EPS, 1.0, m1.var)

            dve.wait_ge(edge_ready, NT)
            second(0)
            for b in range(B):
                if b + 1 < B:
                    second(b + 1)
                third(b)
                if b >= 1:
                    x_norm(b - 1, m1.rstd, m1.xn_ready)
            x_norm(B - 1, m1.rstd, m1.xn_ready)
            route(m1)

            hidden(m1, 0, 0, m1.half)
            hidden(m1, 1, 1, m1.half)
            for i in range(NT):
                copy_hT(m1, i, i % 2)
                if i >= NT - 3:
                    copy_xT(m1, i - (NT - 3), (i - (NT - 3)) % 2)
                hidden(m1, i + 2, i % 2, m1.half)
                dve.wait_ge(m1.y_done, i + 1)
                nc.vector.scalar_tensor_tensor(out=xs[:, i, :], in0=psum[7][:, 0:H], scalar=tg[:, 3:4],
                                               in1=xs[:, i, :], op0=ALU.mult, op1=ALU.add).then_inc(m1.z_added, 1)

            def step1(s, r):
                copy_hT(m1, s + NT, r)
                if below(s, m1.S - 3):
                    copy_xT(m1, s + 3, (r + 1) % 2)
                if below(s, m1.S - 2):
                    hidden(m1, s + (NT + 2), r % 2, m1.half)

            steps(dve, step1, m1.S, m1.S - 3)
            for b in range(B):
                combine(m1, b)

        @block.tensor
        def _(pe):
            mm = nc.tensor.matmul

            def turn(dst, src):
                return nc.tensor.transpose(dst, src, cf[:, C_ID:C_ID + P])

            pe.wait_ge(small_here, 16)
            ctx_all = small_sb[0:D + 1, M_CTX:M_CTX + T]
            wk = small_sb[0:D + 1, M_WK:M_WK + D]
            for h in range(2):
                mm(psum[3 + h][0:D, :], wk, ctx_all[:, h * 512:(h + 1) * 512], start=True, stop=True).then_inc(kvT_done, 1)
            for i in range(NT):
                last = mm(psum[5][:, i * D:(i + 1) * D], ctx_all[:, i * P:(i + 1) * P], wk, start=True, stop=True)
            last.then_inc(kv_done, 1)
            pe.wait_ge(const_here, 16)

            def turn_p(i):
                pe.wait_ge(p_ready, i + 1)
                since(pe, pT_copied, i - 1)
                for k in range(KH):
                    last = turn(psum[i % 2][:, k * P:(k + 1) * P], xn[:, i, k * P:(k + 1) * P])
                last.then_inc(pT_done, 1)

            def attend(i):
                if i == 0:
                    pe.wait_ge(kv_copied, 1)
                pe.wait_ge(pT_copied, i + 1)
                since(pe, oT_copied, i)
                for k in range(KH):
                    last = mm(psum[2][0:D, 0:P], kv[:, 2 * (i // 2) + k, :], pT[:, i % 2, k * P:(k + 1) * P],
                              start=(k == 0), stop=(k == KH - 1))
                last.then_inc(oT_done, 1)

            def score(i):
                if i == 0:
                    pe.wait_ge(kvT_copied, 2)
                pe.wait_ge(oT_copied, i + 1)
                since(pe, s_read, i - 3)
                b = i // 2
                mm(psum[SCORES[i % 4]][:, 0:N], oT[:, i, :], kvT[:, b * N:(b + 1) * N], start=True,
                   stop=True).then_inc(sim_done, 1)

            def turn_xn(m, i):
                pe.wait_ge(m.xn_ready, i + 1)
                since(pe, m.xnT_copied, i)
                for k in range(KH):
                    last = turn(psum[6][:, k * P:(k + 1) * P], xn[:, i, k * P:(k + 1) * P])
                last.then_inc(m.xnT_done, 1)

            def logits(m, i, src):
                pe.wait_ge(m.xnT_copied, i + 1)
                rw = router_sb[:, :, 0:E0] if m.n == 0 else router_sb[:, :, E0:E0 + E1]
                for k in range(KH):
                    last = mm(m.logits[:, i, :], src[:, k * P:(k + 1) * P], rw[:, k, :],
                              start=(k == 0), stop=(k == KH - 1))
                last.then_inc(m.logits_done, 1)

            def ranks(m):
                pe.wait_ge(m.picked, 1)
                mm(m.ranks, ch[:, H_TRI:H_TRI + P], m.A, start=True, stop=False)
                for i in range(NT):
                    last = mm(m.ranks[:, i + 1:NT + 1, :], ch[:, H_ONE:H_ONE + P],
                              m.A[:, i:i + 1, :].to_broadcast([P, NT - i, m.E]), start=False, stop=(i == NT - 1))
                last.then_inc(m.ranks_done, 1)

            def inverse(m):
                for i in range(2 * NT):
                    pe.wait_ge(m.onehots_ready, i + 1)
                    last = mm(m.inverse, lo1[:, i, :], hi2[:, i, :, 0:m.S], start=(i == 0), stop=(i == 2 * NT - 1))
                last.then_inc(m.inverse_done, 1)

            turn_p(0)
            for i in range(NT):
                if i + 1 < NT:
                    turn_p(i + 1)
                attend(i)
                if 1 <= i <= 4:
                    score(i - 1)
            score(4)
            score(5)
            pe.wait_ge(router_here, 16)
            for i in range(NT):
                if i == 2:
                    score(6)
                    score(7)
                turn_xn(mix[0], i)
                logits(mix[0], i, xT[:, i % 2, :])
            pe.wait_ge(constb_here, 16)
            ranks(mix[0])
            inverse(mix[0])
            wj = small_sb[0:D + 1, M_WJ:M_WJ + P]
            wi = small_sb[0:D + 1, M_WI:M_WI + 1]
            pe.wait_ge(s_read, NT)
            for h in range(2):
                mm(psum[4 + h][:, :], wj, ctx_all[:, h * 512:(h + 1) * 512], start=True, stop=True).then_inc(sj_done, 1)
            for i in range(NT):
                last = mm(psum[2][:, i:i + 1], ctx_all[:, i * P:(i + 1) * P], wi, start=True, stop=True)
            last.then_inc(si_done, 1)

            def turn_x(m, t, r):
                pe.wait_ge(m.x_loaded[r], landed(t, r))
                since(pe, m.xT_copied, t)
                for k in range(KH):
                    last = turn(psum[6][:, k * P:(k + 1) * P], x_in[:, r, k * P:(k + 1) * P])
                last.then_inc(m.xT_done, 1)

            def turn_h(m, s, r):
                base = 0 if m.n == 0 else r * F1
                pe.wait_ge(m.h_made, (s + 1) * (2 if m.n == 0 else 1))
                for j, n in m.kf:
                    bank, col = (4, j * P) if j < m.split else (5, (j - m.split) * P)
                    last = nc.tensor.transpose(psum[bank][0:n, col:col + P],
                                               hh[:, base + j * P:base + j * P + n], cf[:, C_ID:C_ID + P])
                last.then_inc(m.hT_done, 1)

            def down(m, s, wd):
                pe.wait_ge(m.hT_copied_a, s + 1)
                pe.wait_ge(m.hT_copied_v, s + 1)
                for j, n in m.kf:
                    last = mm(psum[7][:, 0:H], hT[0:n, j * P:(j + 1) * P], wd(j, n),
                              start=(j == 0), stop=(j == len(m.kf) - 1))
                last.then_inc(m.y_done, 1)

            m = mix[0]

            def owner(m, t):
                return pe.value_load(m.owner[0:1, bass.ds(t, 1)], min_val=0, max_val=m.E - 1)

            def gate_up0(t, r):
                at = owner(m, t) * GU0
                pe.wait_ge(m.xT_copied, t + 1)
                for c in range(2):
                    since(pe, m.h_made, 2 * (t - 1) + c + 1)
                    for g in range(2):
                        for k in range(KH):
                            last = mm(psum[2 * c + g][:, 0:CH0], xT[:, r, k * P:(k + 1) * P],
                                      wgu[:, bass.ds(at + (k * 4 + 2 * c + g) * CH0, CH0)],
                                      start=(k == 0), stop=(k == KH - 1))
                    last.then_inc(m.gu_done, 1)

            def down0(s, r):
                at = owner(m, s) * WD0
                since(pe, m.y_copied, s)
                down(m, s, lambda j, n: wdn[0:n, bass.ds(at + j * H, H)])

            pe.wait_ge(edge_th, NT)
            pe.wait_ge(m.experts_ready, 1)
            turn_x(m, 0, 0)
            pe.wait_ge(w0_here[0], 48)
            gate_up0(0, 0)
            turn_x(m, 1, 1)

            def step0(s, r):
                turn_h(m, s, r)
                if isinstance(s, int) and s < RING:
                    for n in ([s + 1] if s < RING - 1 else range(RING, E0)):
                        pe.wait_ge(w0_here[n], 48)
                if below(s, m.S - 1):
                    gate_up0(s + 1, (r + 1) % 2)
                if below(s, m.S - 2):
                    turn_x(m, s + 2, (r + 2) % RING)
                down0(s, r)

            steps(pe, step0, m.S, m.S - 2)

            m1 = mix[1]

            def gate_up1(t, r, src, at):
                since(pe, m1.h_made, t - 1)
                for k in range(KH):
                    last = mm(psum[r][:, 0:2 * F1], src[:, k * P:(k + 1) * P],
                              wgu[:, bass.ds(at + k * 2 * F1, 2 * F1)], start=(k == 0), stop=(k == KH - 1))
                last.then_inc(m1.gu_done, 1)

            def gate_up_slots(t, r):
                at = owner(m1, t) * GU1 + GU1
                pe.wait_ge(m1.xT_copied, t + 1)
                gate_up1(t + NT, r, xT[:, r, :], at)

            pe.wait_ge(mix[0].y_copied, S0)
            for i in range(NT):
                turn_xn(m1, i)
                logits(m1, i, xnT[:, i, :])
            for n, (_, gu_a, gu_z, dn_a, dn_z) in enumerate(second_weights()):
                pe.wait_ge(w1_here[n], 16 * (gu_z > gu_a) + 32 * (dn_z > dn_a))
            for i in range(2):
                gate_up1(i, i, xnT[:, i, :], SHARED)
            ranks(m1)
            inverse(m1)
            for i in range(NT):
                turn_h(m1, i, i % 2)
                if i + 2 < NT:
                    gate_up1(i + 2, i % 2, xnT[:, i + 2, :], SHARED)
                else:
                    if i + 2 == NT:
                        pe.wait_ge(m1.experts_ready, 1)
                    gate_up_slots(i + 2 - NT, i % 2)
                if i >= NT - 3:
                    turn_x(m1, i - (NT - 3), i - (NT - 3))
                since(pe, m1.z_added, i)
                down(m1, i, lambda j, n: wdn[0:n, j * H:(j + 1) * H])

            def step1(s, r):
                turn_h(m1, s + NT, r % 2)
                if below(s, m1.S - 2):
                    gate_up_slots(s + 2, r % 2)
                if below(s, m1.S - 3):
                    turn_x(m1, s + 3, (r + 3) % RING)
                if isinstance(s, int) and s == 0:
                    pe.wait_ge(m1.z_added, NT)
                at = owner(m1, s) * WD1 + WD1
                since(pe, m1.y_copied, s)
                down(m1, s + NT, lambda j, n: wdn[0:n, bass.ds(at + j * H, H)])

            steps(pe, step1, m1.S, m1.S - 3)


def _constants():
    import numpy as np
    c = np.zeros((P, C_ALL), np.float32)
    c[:, C_ID:C_ID + P] = np.eye(P)
    c[:, C_DESC:C_DESC + 16] = 16 - np.arange(16)
    c[:, C_THR:C_THR + NT - 1] = P * np.arange(1, NT)
    c[:, C_LT:C_LT + E1 * E1] = np.tril(np.ones((E1, E1)), -1).ravel()
    c[:, C_SLOT:C_SLOT + S1] = np.arange(S1)
    c[:, C_NH] = -0.5
    token = P * np.arange(NT)[None, :, None] + np.arange(P)[:, None, None]
    token, pick = np.broadcast_arrays(token[:, None], np.arange(2)[None, :, None, None])
    c[:, C_VAL:C_VAL + 4 * NT] = np.concatenate([token, 2 * token + pick + 1], 3).reshape(P, 4 * NT)
    c[:, C_PAD:C_PAD + S1] = 2 * T + 1 + P * np.arange(S1)[None] + np.arange(P)[:, None]
    half = np.concatenate([np.triu(np.ones((P, P)), 1), np.ones((P, P)),
                           np.broadcast_to(np.arange(P), (P, P))], 1)
    return c, half.astype(np.float16)


def kernel(**inputs):
    import numpy as np
    import concourse.bacc as bacc
    from concourse.bass_utils import run_bass_kernel_spmd

    a = {k: np.asarray(v) for k, v in inputs.items()}
    f32 = np.float32
    const_f, const_h = _constants()

    small = np.zeros((M_ROWS, M_ALL), f32)
    small[0:D, M_CTX:M_CTX + T] = a["ctx_512"].reshape(T, D).T
    small[D, M_CTX:M_CTX + T] = 1.0
    small[0:D, M_WK:M_WK + D] = a["L0_xattn_W_k"].T
    small[D, M_WK:M_WK + D] = a["L0_xattn_b_k"]
    small[0:D, M_WJ:M_WJ + P] = a["L1_xattn_W"][0, D:, None]
    small[D, M_WJ:M_WJ + P] = a["L1_xattn_b"][0]
    small[0:D, M_WI] = a["L1_xattn_W"][0, :D]
    vecs = np.concatenate([a["L0_xattn_ln_gamma"], a["L0_xattn_ln_beta"], a["g_xattn"], a["g_ffn"]])[None]
    router = np.concatenate([a["L0_ffn_router_w"], a["L1_ffn_gate_w"]], 0).T.reshape(KH, P, E0 + E1)

    def split(w, halves):
        e, f, _ = w.shape
        return w.reshape(e, halves, f // halves, KH, P).transpose(0, 4, 3, 1, 2)

    def shared_first(w, s):
        return np.concatenate([s[None], w], 0)

    gu0 = np.stack([split(a["L0_ffn_gate_w"], 2), split(a["L0_ffn_up_w"], 2)], 4)
    gu1 = np.stack([split(shared_first(a["L1_ffn_w1"], a["L1_ffn_sw1"]), 1),
                    split(shared_first(a["L1_ffn_w3"], a["L1_ffn_sw3"]), 1)], 4)
    d0 = a["L0_ffn_down_w"].transpose(0, 2, 1)
    d1 = shared_first(a["L1_ffn_w2"], a["L1_ffn_sw2"]).transpose(0, 2, 1)
    cut = (len(KF0) - 1) * P
    arrays = {
        "x": a["x"].reshape(T, H), "small": small, "vecs": vecs, "router": router.transpose(1, 0, 2),
        "const_f": const_f, "const_h": const_h,
        "gu0": gu0.reshape(E0, P, GU0),
        "wd0a": d0[:, :cut].reshape(E0, cut // P, P, H).transpose(0, 2, 1, 3).reshape(E0, P, cut // P * H),
        "wd0b": d0[:, cut:],
        "gu1": gu1.reshape(E1 + 1, P, GU1), "wd1a": d1[:, :P], "wd1b": d1[:, P:],
    }
    arrays = {k: np.ascontiguousarray(v) for k, v in arrays.items()}
    nc = bacc.Bacc("TRN2", target_bir_lowering=False, num_devices=1)
    aps = [nc.dram_tensor(k, v.shape, mybir.dt.from_np(v.dtype), kind="ExternalInput").ap() for k, v in arrays.items()]
    out = nc.dram_tensor("out", (T, H), mybir.dt.float32, kind="ExternalOutput").ap()
    build(nc, *aps, out)
    r = run_bass_kernel_spmd(nc, [arrays], core_ids=[0])
    return r.results[0]["out"].reshape(B, N, H)
```

```python
import concourse.bass as bass
from concourse import mybir
from contextlib import ExitStack

P = 128
B, N, H, D = 4, 256, 256, 64
T = B * N
NT = T // P
KH = H // P
E0, F0 = 8, 688
E1, F1 = 15, 176
SHARED = 0


def most_tiles(experts):
    return min(experts * (T // P), (2 * T + (P - 1) * experts) // P)


S0, S1 = most_tiles(E0), most_tiles(E1)
KF0 = [(j, min(P, F0 - j * P)) for j in range(-(-F0 // P))]
KF1 = [(j, min(P, F1 - j * P)) for j in range(-(-F1 // P))]
CH0 = F0 // 2
GU0, GU1 = KH * 2 * F0, KH * 2 * F1
WD0, WD1 = len(KF0) * H, len(KF1) * H
GUALL = E0 * GU0
WDALL = E0 * WD0


def second_weights():
    had_gu = had_dn = 0
    for k in range(1, E0):
        gu, dn = min(E1 + 1, k * GU0 // GU1), min(E1 + 1, k * WD0 // WD1)
        if gu > had_gu or dn > had_dn:
            yield k, had_gu, gu, had_dn, dn
        had_gu, had_dn = gu, dn


C_ID = 0
C_DESC = C_ID + P
C_THR = C_DESC + 16
C_LT = C_THR + NT
C_SLOT = C_LT + E1 * E1
C_NH = C_SLOT + S1
C_VAL = C_NH + 1
C_PAD = C_VAL + 4 * NT
C_ALL = C_PAD + S1
H_TRI, H_ONE, H_LO, H_ALL = 0, P, 2 * P, 3 * P
EARLY = 3
RING = 4

M_CTX = 0
M_WK = M_CTX + T
M_WJ = M_WK + D
M_WI = M_WJ + P
M_ALL = M_WI + 1
M_ROWS = 80

V_GAMMA, V_BETA, V_GX, V_GF = 0, N, 2 * N, 2 * N + 2
V_ALL = 2 * N + 4

LN_EPS = 1e-5
SIM_EPS = 1e-6
SIM_SCALE = float(N) ** -0.5
NEVER = -3.0e38


def build(nc, x, small, vecs, router, const_f, const_h, gu0, wd0a, wd0b, gu1, wd1a, wd1b, out):
    fp32, fp16, i32 = mybir.dt.float32, mybir.dt.float16, mybir.dt.int32
    ALU = mybir.AluOpType
    ACT = mybir.ActivationFunctionType
    X = mybir.AxisListType.X

    rows = nc.dram_tensor("rows", (T, H), fp32).ap()
    results = nc.dram_tensor("results", (2 * T + S1 * P, H), fp32).ap()
    rows_t = rows.rearrange("(i p) h -> p i h", p=P)
    results_t = results[0:2 * T, :].rearrange("(i p k) h -> p i (k h)", p=P, k=2)
    x_t = x.rearrange("(i p) h -> p i h", p=P)
    out_t = out.rearrange("(i p) h -> p i h", p=P)

    ctx = ExitStack()
    with ctx:
        def sb(name, shape, dt=fp32):
            return ctx.enter_context(nc.sbuf_tensor(name, shape, dt))

        def sem(name):
            return ctx.enter_context(nc.semaphore(name))

        wgu = sb("wgu", [P, GUALL])
        wdn = sb("wdn", [P, WDALL])
        xs = sb("xs", [P, NT, H])
        xn = sb("xn", [P, NT, H])
        edge = sb("edge", [P, NT, H])
        small_sb = sb("small_sb", [M_ROWS, M_ALL])
        vec_sb = sb("vec_sb", [P, V_ALL])
        router_sb = sb("router_sb", [P, KH, E0 + E1])
        cf = sb("cf", [P, C_ALL])
        ch = sb("ch", [P, H_ALL], fp16)
        gamma16 = sb("gamma16", [P, N])
        tg = sb("tg", [P, 4])
        edge_c = sb("edge_c", [P, 2])
        lower = sb("lower", [P, 2 * T])
        kvT = lower[0:D, 0:T]
        kv = sb("kv", [P, NT, D])
        half_si = sb("half_si", [P, NT])
        half_b = sb("half_b", [P, NT])
        pT = sb("pT", [P, 2, H])
        oT = lower[0:D, T:2 * T].rearrange("p (i n) -> p i n", n=P)
        z = sb("z", [P, 4, N])
        e = sb("e", [P, 2, N])
        st = sb("st", [P, NT, 6])
        mv = sb("mv", [P, NT, 2])
        ve = sb("ve", [P, NT])
        rs = sb("rs", [P, NT])
        mx = sb("mx", [P, NT])
        nmx = sb("nmx", [P, NT])
        sm = sb("sm", [P, NT])
        rc = sb("rc", [P, NT])
        cc = sb("cc", [P, NT])
        off = sb("off", [P, NT])
        x_in = sb("x_in", [P, RING, H])
        xT = sb("xT", [P, 2, H])
        th = sb("th", [P, F0])
        hh = sb("hh", [P, F0])
        hT = sb("hT", [P, len(KF0) * P])
        y_sb = sb("y_sb", [P, RING, H])
        lo1 = z[:].bitcast(fp16).rearrange("p a b -> p (a b)").rearrange("p (i n) -> p i n", n=P)
        hi1 = pT[:].bitcast(fp16).rearrange("p a b -> p (a b)")[:, 0:2 * NT * S1].rearrange("p (i s) -> p i s", s=S1)
        hi2 = e[:].bitcast(fp16).rearrange("p a b -> p (a b)")[:, 0:4 * NT * S1].rearrange(
            "p (i q s) -> p i q s", q=2, s=S1)
        val16 = sb("val16", [P, 2 * NT, 2], fp16)
        gu_copy = y_sb[:].rearrange("p r h -> p (r h)")[:, 0:4 * F1].rearrange("p (r f) -> p r f", f=2 * F1)
        free = (E1 + 1) * GU1
        y_got = wgu[:, free:free + 2 * NT * H].rearrange("p (i k h) -> p i k h", k=2, h=H)
        xnT = wgu[:, free + 2 * NT * H:free + 3 * NT * H].rearrange("p (i h) -> p i h", h=H)

        psum = [ctx.enter_context(nc.psum_tensor(f"bank{i}", [P, 512], fp32)) for i in range(8)]
        ident = cf[:, C_ID:C_ID + P]

        x_here = [sem(f"x_here{i}") for i in range(B)]
        small_here, vec_here, router_here = sem("small_here"), sem("vec_here"), sem("router_here")
        const_here, constb_here = sem("const_here"), sem("constb_here")
        w0_here = [sem(f"w0_here{i}") for i in range(E0)]
        w1_here = [sem(f"w1_here{i}") for i, _ in enumerate(second_weights())]
        out_stored = sem("out_stored")
        kvT_done, kv_done, kvT_copied, kv_copied = sem("kvT_done"), sem("kv_done"), sem("kvT_copied"), sem("kv_copied")
        gates_done = sem("gates_done")
        p_var, p_rstd, p_ready = sem("p_var"), sem("p_rstd"), sem("p_ready")
        pT_done, pT_copied = sem("pT_done"), sem("pT_copied")
        oT_done, oT_copied, sim_done = sem("oT_done"), sem("oT_copied"), sem("sim_done")
        s_var, s_rstd, s_terms, s_read, z_scaled = (
            sem("s_var"), sem("s_rstd"), sem("s_terms"), sem("s_read"), sem("z_scaled"))
        gamma_ready, z_ready, exp_done = sem("gamma_ready"), sem("z_ready"), sem("exp_done")
        dve_step = sem("dve_step")
        first_scaled, first_added = sem("first_scaled"), sem("first_added")
        x2_var, x2_rstd = sem("x2_var"), sem("x2_rstd")
        mix_ready, mixed = sem("mix_ready"), sem("mixed")
        half_shared, gu_copied, z_copied, z_added = (
            sem("half_shared"), sem("gu_copied"), sem("z_copied"), sem("z_added"))
        sj_done, si_done, si_copied, edge_th, edge_c_ready, edge_ready = (
            sem("sj_done"), sem("si_done"), sem("si_copied"), sem("edge_th"), sem("edge_c_ready"), sem("edge_ready"))

        kept, filled = {}, [0]
        LARGEST = {"oh": 2 * NT * E1, "w12": 2 * NT * E1, "A": (NT + 1) * E1, "cmp": E1 * NT,
                   "lt": E1 * E1, "scmp": S1 * (E1 - 1), "place": 2 * NT, "lo": 2 * NT, "hi": 2 * NT, "lof": 2 * NT,
                   "L2": NT * E1, "w": NT * E1, "R2": NT * E1}
        STAY = ("c1", "c2", "tok", "dst", "owner")

        def work(name, *shape, dt=fp32):
            if name not in kept:
                most = LARGEST.get(name, S1)
                if name == "scmp":
                    kept[name] = lower[:, 0:most]
                elif name in STAY:
                    kept[name] = sb("route_" + name, [P, most], dt)
                else:
                    flat = lower[:, filled[0]:filled[0] + most]
                    filled[0] += most
                    kept[name] = flat if dt == fp32 else flat.bitcast(dt)
            size = 1
            for x in shape:
                size *= x
            flat = kept[name][:, 0:size]
            if len(shape) == 1:
                return flat
            if len(shape) == 2:
                return flat.rearrange("p (a b) -> p a b", b=shape[1])
            return flat.rearrange("p (a b c) -> p a b c", b=shape[1], c=shape[2])

        class Mixture:

            def __init__(m, n, experts, tiles, kf, chunk, ahead):
                m.split = 4 if n == 0 else 1
                m.n, m.E, m.S, m.kf, m.ahead = n, experts, tiles, kf, ahead
                m.logits = [psum[6][:, 0:(NT - 2) * experts].rearrange("p (i e) -> p i e", e=experts),
                            psum[2 + n][:, 0:2 * experts].rearrange("p (i e) -> p i e", e=experts)]
                m.ranks = psum[0 if n == 0 else 2][:, 0:(NT + 1) * experts].rearrange("p (i e) -> p i e", e=experts)
                m.inverse = psum[3][:, 0:2 * tiles].rearrange("p (q s) -> p q s", q=2)
                m.terms = sem(f"terms{n}")
                m.var, m.rstd, m.xn_ready = sem(f"var{n}"), sem(f"rstd{n}"), sem(f"xn_ready{n}")
                m.xnT_done, m.xnT_copied = sem(f"xnT_done{n}"), sem(f"xnT_copied{n}")
                m.logits_done, m.picked = sem(f"logits_done{n}"), sem(f"picked{n}")
                m.shifted, m.exps = sem(f"shifted{n}"), sem(f"exps{n}")
                m.ranks_done = sem(f"ranks_done{n}")
                m.onehots_ready, m.inverse_done = sem(f"onehots_ready{n}"), sem(f"inverse_done{n}")
                m.tokens_ready, m.targets_ready = sem(f"tokens_ready{n}"), sem(f"targets_ready{n}")
                m.experts_ready = sem(f"experts_ready{n}")
                m.rows_stored = sem(f"rows_stored{n}")
                m.x_loaded = [sem(f"x_loaded{n}{r}") for r in range(RING)]
                m.xT_done, m.xT_copied = sem(f"xT_done{n}"), sem(f"xT_copied{n}")
                m.gu_done, m.th_done, m.h_made = sem(f"gu_done{n}"), sem(f"th_done{n}"), sem(f"h_made{n}")
                m.hT_done = sem(f"hT_done{n}")
                m.hT_copied_a, m.hT_copied_v = sem(f"hT_copied_a{n}"), sem(f"hT_copied_v{n}")
                m.y_done, m.y_copied = sem(f"y_done{n}"), sem(f"y_copied{n}")
                m.y_stored = [sem(f"y_stored{n}{r}") for r in range(RING)]
                m.y_here = [sem(f"y_here{n}{b}") for b in range(B)]
                m.x_new = sem(f"x_new{n}")
                m.half = sem(f"half{n}")
                W, k2 = experts, 2 * NT
                m.oh, m.w12 = work("oh", 2, NT, W), work("w12", 2, NT, W)
                m.L2, m.w, m.R2 = (work(x, NT, W) for x in ("L2", "w", "R2"))
                m.A = work("A", NT + 1, W, dt=fp16)
                m.place, m.lo, m.hi = (work(x, k2, dt=i32) for x in ("place", "lo", "hi"))
                m.lof = work("lof", k2)
                m.tok, m.dst, m.pad = work("tok", tiles, dt=i32), work("dst", tiles, dt=i32), work("pad", tiles)
                m.v1, m.v2, m.m, m.d, m.ed = (work(x, NT) for x in ("v1", "v2", "m", "d", "ed"))
                m.den, m.p1, m.c1, m.c2 = (work(x, NT) for x in ("den", "p1", "c1", "c2"))
                m.cmp, m.lt = work("cmp", W, NT), work("lt", W, W)
                m.tl, m.base, m.incl = work("tl", W), work("base", W), work("incl", W)
                m.scmp, m.ownf = work("scmp", tiles, W - 1), work("ownf", tiles)
                m.owner = work("owner", tiles, dt=i32)

        mix = [Mixture(0, E0, S0, KF0, CH0, 1), Mixture(1, E1, S1, KF1, F1, 2)]

        def steps(eng, step, total, full):
            for s in range(RING):
                step(s, s)
            groups = full // RING
            with eng.Fori(1, groups) as j:
                for r in range(RING):
                    step(j * RING + r, r)
            for s in range(RING * groups, total):
                step(s, s % RING)

        def landed(n, r):
            return n * (16 // RING) + (16 - 16 // RING * r)

        def since(eng, semaphore, value):
            if not isinstance(value, int) or value > 0:
                eng.wait_ge(semaphore, value)

        def below(s, limit):
            return not isinstance(s, int) or s < limit

        SCORES = (3, 4, 5, 7)

        block = ctx.enter_context(nc.Block())

        @block.sync
        def _(sp):
            for b in range(B):
                sp.dma_start(xs[:, 2 * b:2 * b + 2, :], x_t[:, 2 * b:2 * b + 2, :]).then_inc(x_here[b], 16)
            sp.dma_start(router_sb[:], router).then_inc(router_here, 16)
            sp.dma_start(ch[:], const_h).then_inc(constb_here, 16)
            for n in range(E0):
                sp.dma_start(wgu[:, n * GU0:(n + 1) * GU0], gu0[n]).then_inc(w0_here[n], 16)
                tail = KF0[-1][0] * H
                sp.dma_start(wdn[:, n * WD0:n * WD0 + tail], wd0a[n]).then_inc(w0_here[n], 16)
                sp.dma_start(wdn[0:KF0[-1][1], n * WD0 + tail:(n + 1) * WD0], wd0b[n]).then_inc(w0_here[n], 16)
            for m in mix:
                for b in range(B):
                    sp.wait_ge(m.xn_ready, 2 * b + 2)
                    sp.dma_start(rows_t[:, 2 * b:2 * b + 2, :], xn[:, 2 * b:2 * b + 2, :]).then_inc(m.rows_stored, 16)
                if m is mix[0]:
                    for n, (k, gu_a, gu_z, dn_a, dn_z) in enumerate(second_weights()):
                        sp.wait_ge(mix[0].y_done, most_tiles(k))
                        if gu_z > gu_a:
                            sp.dma_start(
                                wgu[:, gu_a * GU1:gu_z * GU1].rearrange("p (e n) -> p e n", n=GU1),
                                gu1[gu_a:gu_z].rearrange("e p n -> p e n")).then_inc(w1_here[n], 16)
                        if dn_z > dn_a:
                            dn = wdn[:, dn_a * WD1:dn_z * WD1].rearrange("p (e n) -> p e n", n=WD1)
                            sp.dma_start(dn[:, :, 0:H], wd1a[dn_a:dn_z].rearrange("e p n -> p e n")
                                                ).then_inc(w1_here[n], 16)
                            sp.dma_start(dn[0:KF1[1][1], :, H:2 * H], wd1b[dn_a:dn_z].rearrange("e p n -> p e n")
                                                ).then_inc(w1_here[n], 16)
                for r in range(RING):
                    last = (m.S - 1 - r) // RING * RING + r
                    sp.wait_ge(m.y_stored[r], landed(last, r))
                for b in range(B):
                    sp.dma_start(y_got[:, 2 * b:2 * b + 2, :, :].rearrange("p i k h -> p i (k h)"),
                                 results_t[:, 2 * b:2 * b + 2, :]).then_inc(m.y_here[b], 16)
            for i in range(NT):
                sp.wait_ge(mix[1].x_new, i + 1)
                sp.dma_start(out_t[:, i, :], xs[:, i, :]).then_inc(out_stored, 16)
            sp.wait_ge(out_stored, 16 * NT)

        @block.gpsimd
        def _(pool):
            minus_half = cf[:, C_NH:C_NH + 1].to_broadcast([P, 2])
            pool.wait_ge(const_here, 16)

            def rstd(b, var, ready):
                pool.wait_ge(var, b + 1)
                nc.gpsimd.tensor_tensor(rs[:, 2 * b:2 * b + 2], ve[:, 2 * b:2 * b + 2], minus_half,
                                        ALU.pow).then_inc(ready, 1)

            def scale_z(i):
                pool.wait_ge(s_read, i + 1)
                nc.gpsimd.tensor_tensor(z[:, i % 4, :], z[:, i % 4, :], gamma16[:], ALU.mult).then_inc(z_scaled, 1)

            for b in range(B):
                rstd(b, p_var, p_rstd)
            rstd(0, s_var, s_rstd)
            pool.wait_ge(gamma_ready, 1)
            for b in range(B):
                scale_z(2 * b)
                scale_z(2 * b + 1)
                if b >= 1:
                    rstd(b - 1, mix[0].var, mix[0].rstd)
                if b + 1 < B:
                    rstd(b + 1, s_var, s_rstd)
            rstd(B - 1, mix[0].var, mix[0].rstd)

            def gather(m, t):
                nc.gpsimd.indirect_dma_start(
                    out=x_in[:, t % RING, :], out_offset=None, in_=rows,
                    in_offset=bass.IndirectOffsetOnAxis(ap=m.tok[:, t:t + 1], axis=0)).then_inc(m.x_loaded[t % RING], 16)

            def scatter(m, s):
                nc.gpsimd.indirect_dma_start(
                    out=results, out_offset=bass.IndirectOffsetOnAxis(ap=m.dst[:, s:s + 1], axis=0),
                    in_=y_sb[:, s % RING, :], in_offset=None).then_inc(m.y_stored[s % RING], 16)

            def ready_to_gather(m):
                pool.wait_ge(m.tokens_ready, 1)
                pool.wait_ge(m.rows_stored, 16 * B)

            def exchange(m, begun, extra):
                lead = m.ahead + 1 + RING
                for t in range(begun, lead):
                    since(pool, m.xT_done, t - RING + 1)
                    gather(m, t)
                pool.wait_ge(m.targets_ready, 1)
                for s in range(m.S):
                    if s + lead < m.S:
                        pool.wait_ge(m.xT_done, s + lead - RING + 1)
                        gather(m, s + lead)
                    pool.wait_ge(m.y_copied, s + 1)
                    scatter(m, s)
                    extra(s)

            pool.wait_ge(edge_c_ready, 1)

            def finish_edge(s):
                if s < RING:
                    for i in range(2 * s, 2 * s + 2):
                        pool.wait_ge(edge_th, i + 1)
                        nc.gpsimd.tensor_scalar(edge[:, i, :], edge[:, i, :], edge_c[:, 0:1], edge_c[:, 0:1],
                                                ALU.mult, ALU.add).then_inc(edge_ready, 1)

            ready_to_gather(mix[0])
            exchange(mix[0], 0, finish_edge)
            def add_first(b):
                for i in (2 * b, 2 * b + 1):
                    pool.wait_ge(first_scaled, i - 1)
                    nc.gpsimd.tensor_tensor(xs[:, i, :], xs[:, i, :], y_got[:, i, 0, :], ALU.add).then_inc(first_added, 1)

            add_first(1)
            rstd(0, x2_var, x2_rstd)
            add_first(2)
            rstd(1, x2_var, x2_rstd)
            add_first(3)
            for b in range(B):
                if b + 2 < B:
                    rstd(b + 2, x2_var, x2_rstd)
                rstd(b, mix[1].var, mix[1].rstd)

            m1 = mix[1]

            def hidden_shared(i):
                cols = slice(i % 2 * F1, (i % 2 + 1) * F1)
                pool.wait_ge(gu_copied, 2 * i + 2)
                since(pool, m1.hT_done, i - 1)
                nc.gpsimd.tensor_tensor(hh[:, cols], th[:, cols], gu_copy[:, i % 2, 0:F1],
                                        ALU.mult).then_inc(half_shared, 1)
                pool.wait_ge(half_shared, i + 1)
                nc.gpsimd.tensor_tensor(hh[:, cols], hh[:, cols], gu_copy[:, i % 2, F1:2 * F1],
                                        ALU.mult).then_inc(m1.h_made, 1)

            hidden_shared(0)
            hidden_shared(1)
            for i in range(NT):
                if i + 2 < NT:
                    hidden_shared(i + 2)
                pool.wait_ge(z_copied, i + 1)
                nc.gpsimd.tensor_tensor(xs[:, i, :], edge[:, i, :], xs[:, i, :], ALU.add).then_inc(z_added, 1)
                if i >= EARLY:
                    if i == EARLY:
                        ready_to_gather(m1)
                    gather(m1, i - EARLY)
            exchange(m1, NT - EARLY, lambda s: None)

        @block.scalar
        def _(act):
            act.dma_start(cf[:], const_f).then_inc(const_here, 16)
            act.dma_start(small_sb[:], small).then_inc(small_here, 16)
            act.dma_start(vec_sb[:], vecs.to_broadcast([P, V_ALL])).then_inc(vec_here, 16)
            act.wait_ge(vec_here, 16)
            nc.scalar.activation(tg[:], vec_sb[:, V_GX:V_GX + 4], ACT.Tanh).then_inc(gates_done, 1)
            act.wait_ge(kv_done, 1)
            nc.scalar.activation(kv[:].rearrange("p i d -> p (i d)"), psum[5][:, :], ACT.Copy).then_inc(kv_copied, 1)

            def copy_keys(h):
                act.wait_ge(kvT_done, h + 1)
                nc.scalar.activation(kvT[:, h * 512:(h + 1) * 512], psum[3 + 3 * h][0:D, :], ACT.Copy).then_inc(kvT_copied, 1)

            def copy_pT(i):
                act.wait_ge(pT_done, i + 1)
                since(act, oT_done, i - 1)
                nc.scalar.activation(pT[:, i % 2, :], psum[i % 2][:, 0:H], ACT.Copy).then_inc(pT_copied, 1)

            def copy_oT(i):
                act.wait_ge(oT_done, i + 1)
                nc.scalar.activation(oT[:, i, :], psum[2][0:D, 0:P], ACT.Copy).then_inc(oT_copied, 1)

            def exps(b):
                for i in (2 * b, 2 * b + 1):
                    act.wait_ge(z_ready, b + 1)
                    nc.scalar.activation(e[:, i % 2, :], z[:, i % 4, :], ACT.Exp, bias=nmx[:, i:i + 1],
                                         accum_out=sm[:, i:i + 1]).then_inc(exp_done, 1)

            def norm_scores(b):
                act.wait_ge(s_terms, b + 1)
                for i in (2 * b, 2 * b + 1):
                    nc.scalar.activation(z[:, i % 4, :], psum[SCORES[i % 4]][:, 0:N], ACT.Identity,
                                         bias=off[:, i:i + 1], scale=rs[:, i:i + 1]).then_inc(s_read, 1)

            def norm_rows(m, b):
                act.wait_ge(m.terms, b + 1)
                for i in (2 * b, 2 * b + 1):
                    nc.scalar.activation(xn[:, i, :], xs[:, i, :], ACT.Identity, bias=off[:, i:i + 1],
                                         scale=rs[:, i:i + 1]).then_inc(m.xn_ready, 1)

            def copy_xnT(m, i, dst):
                act.wait_ge(m.xnT_done, i + 1)
                nc.scalar.activation(dst, psum[i % 2][:, 0:H], ACT.Copy).then_inc(m.xnT_copied, 1)

            copy_pT(0)
            copy_pT(1)
            copy_keys(0)
            copy_oT(0)
            copy_pT(2)
            copy_oT(1)
            copy_pT(3)
            copy_oT(2)
            copy_keys(1)
            norm_scores(0)
            for i in range(3, NT):
                if i + 1 < NT:
                    copy_pT(i + 1)
                copy_oT(i)
                if i == 5:
                    exps(0)
            norm_scores(1)
            exps(1)

            act.wait_ge(si_done, 1)
            nc.scalar.activation(half_si[:], psum[2][:, 0:NT], ACT.Copy, scale=0.5).then_inc(si_copied, 1)

            def edge_tanh(h):
                act.wait_ge(sj_done, h + 1)
                for i in range(4 * h, 4 * h + 4):
                    if i == 0:
                        act.wait_ge(si_copied, 1)
                    nc.scalar.activation(edge[:, i, :], psum[6 - 5 * h][:, (i // 2 % 2) * N:(i // 2 % 2 + 1) * N],
                                         ACT.Tanh, bias=half_si[:, i:i + 1], scale=0.5).then_inc(edge_th, 1)

            def copy_xnTs0(b):
                for i in (2 * b, 2 * b + 1):
                    copy_xnT(mix[0], i, xT[:, i % 2, :])

            norm_scores(2)
            edge_tanh(0)
            norm_rows(mix[0], 0)
            exps(2)
            norm_scores(3)
            edge_tanh(1)
            copy_xnTs0(0)
            norm_rows(mix[0], 1)
            exps(3)
            copy_xnTs0(1)
            norm_rows(mix[0], 2)
            copy_xnTs0(2)
            norm_rows(mix[0], 3)
            copy_xnTs0(3)

            def route_exps(m):
                act.wait_ge(m.shifted, 1)
                nc.scalar.activation(m.ed, m.d, ACT.Exp).then_inc(m.exps, 1)
                if m.n == 1:
                    nc.scalar.activation(m.L2.rearrange("p i e -> p (i e)"),
                                         m.L2.rearrange("p i e -> p (i e)"), ACT.Exp).then_inc(m.exps, 1)

            route_exps(mix[0])
            def tanh_half(m, t, r):
                if m.n == 0:
                    for c in range(2):
                        act.wait_ge(m.gu_done, 2 * t + c + 1)
                        since(act, m.h_made, 2 * (t - 1) + c + 1)
                        nc.scalar.activation(th[:, c * CH0:(c + 1) * CH0], psum[2 * c][:, 0:CH0], ACT.Tanh,
                                             scale=0.5).then_inc(m.th_done, 1)
                else:
                    act.wait_ge(m.gu_done, t + 1)
                    since(act, m.h_made, t - 1)
                    nc.scalar.activation(th[:, r * F1:(r + 1) * F1], psum[r][:, 0:F1], ACT.Tanh,
                                         scale=0.5).then_inc(m.th_done, 1)

            def copy_hT(m, s, r):
                act.wait_ge(m.hT_done, s + 1)
                n = 512 if m.n == 0 else P
                nc.scalar.activation(hT[:, 0:n], psum[4][:, 0:n], ACT.Copy, scale=0.5).then_inc(m.hT_copied_a, 1)

            m = mix[0]
            tanh_half(m, 0, 0)

            def step0(s, r):
                copy_hT(m, s, r)
                if below(s, m.S - 1):
                    tanh_half(m, s + 1, (r + 1) % 2)
                act.wait_ge(m.y_done, s + 1)
                if not isinstance(s, int) or s >= RING:
                    act.wait_ge(m.y_stored[r], s * 4 - 4 * r)
                nc.scalar.activation(y_sb[:, r, :], psum[7][:, 0:H], ACT.Copy).then_inc(m.y_copied, 1)

            steps(act, step0, m.S, m.S - 1)

            m1 = mix[1]
            def mix_rows(b):
                act.wait_ge(mix_ready, b + 1)
                for i in (2 * b, 2 * b + 1):
                    nc.scalar.activation(xn[:, i, :], xs[:, i, :], ACT.Identity, bias=nmx[:, i:i + 1],
                                         scale=cc[:, i:i + 1]).then_inc(mixed, 1)

            def copy_xnTs(b):
                for i in (2 * b, 2 * b + 1):
                    copy_xnT(m1, i, xnT[:, i, :])

            def scale_first(b):
                act.wait_ge(mix[0].y_here[b], 16)
                for i in (2 * b, 2 * b + 1):
                    nc.scalar.activation(y_got[:, i, 0, :], y_got[:, i, 0, :], ACT.Copy,
                                         scale=mix[0].c1[:, i:i + 1]).then_inc(first_scaled, 1)

            scale_first(1)
            scale_first(2)
            mix_rows(0)
            scale_first(3)
            mix_rows(1)
            mix_rows(2)
            norm_rows(m1, 0)
            mix_rows(3)
            for b in range(1, B):
                norm_rows(m1, b)
                copy_xnTs(b - 1)
            copy_xnTs(B - 1)

            def act_on_shared(i):
                tanh_half(m1, i, i % 2)
                nc.scalar.activation(gu_copy[:, i % 2, :], psum[i % 2][:, 0:2 * F1], ACT.Copy).then_inc(gu_copied, 1)
                cols = slice(i % 2 * F1, (i % 2 + 1) * F1)
                act.wait_ge(m1.th_done, i + 1)
                nc.scalar.activation(th[:, cols], th[:, cols], ACT.Identity,
                                     bias=cf[:, C_SLOT + 1:C_SLOT + 2]).then_inc(gu_copied, 1)

            act_on_shared(0)
            act_on_shared(1)
            for i in range(NT):
                act.wait_ge(m1.hT_done, i + 1)
                nc.scalar.activation(hT[:, 0:P], psum[4][:, 0:P], ACT.Copy, scale=0.5).then_inc(m1.hT_copied_a, 1)
                nc.scalar.activation(hT[0:KF1[-1][1], P:2 * P], psum[5][0:KF1[-1][1], 0:P], ACT.Copy,
                                     scale=0.5).then_inc(m1.hT_copied_v, 1)
                if i + 2 < NT:
                    act_on_shared(i + 2)
                if i == NT - 1:
                    tanh_half(m1, NT, 0)
                act.wait_ge(m1.y_done, i + 1)
                nc.scalar.activation(edge[:, i, :], psum[7][:, 0:H], ACT.Copy, scale=tg[:, 3:4]).then_inc(z_copied, 1)
                if i == 1:
                    route_exps(m1)
            tanh_half(m1, NT + 1, 1)

            def step1(s, r):
                copy_hT(m1, s + NT, r)
                if below(s, m1.S - 2):
                    tanh_half(m1, s + (NT + 2), r % 2)
                act.wait_ge(m1.y_done, s + (NT + 1))
                if not isinstance(s, int) or s >= RING:
                    act.wait_ge(m1.y_stored[r], s * 4 - 4 * r)
                nc.scalar.activation(y_sb[:, r, :], psum[7][:, 0:H], ACT.Copy).then_inc(m1.y_copied, 1)

            steps(act, step1, m1.S, m1.S - 2)

        @block.vector
        def _(dve):
            count = [0]

            def then(instruction):
                count[0] += 1
                instruction.then_inc(dve_step, 1)
                dve.wait_ge(dve_step, count[0])

            def did(instruction):
                count[0] += 1
                instruction.then_inc(dve_step, 1)
                return count[0]

            def after(n):
                dve.wait_ge(dve_step, n)

            def stats(src, b, eps, scale, signal):
                tiles = (2 * b, 2 * b + 1)
                ends = [did(nc.vector.bn_stats(st[:, i, :], src(i))) for i in tiles]
                for i, end in zip(tiles, ends):
                    after(end)
                    last = did(nc.vector.bn_aggr(mv[:, i, :], st[:, i, :]))
                after(last)
                nc.vector.tensor_scalar(ve[:, 2 * b:2 * b + 2], mv[:, 2 * b:2 * b + 2, 1], scale, eps,
                                        ALU.mult, ALU.add).then_inc(signal, 1)

            def rows_of_x(i):
                return xs[:, i, :]

            def x_norm(b, rstd, signal):
                dve.wait_ge(rstd, b + 1)
                for i in (2 * b, 2 * b + 1):
                    nc.vector.tensor_scalar(xn[:, i, :], xs[:, i, :], mv[:, i, 0:1], rs[:, i:i + 1],
                                            ALU.subtract, ALU.mult).then_inc(signal, 1)

            for b in range(B + 1):
                if b < B:
                    dve.wait_ge(x_here[b], 16)
                    stats(rows_of_x, b, LN_EPS, 1.0, p_var)
                if b >= 1:
                    x_norm(b - 1, p_rstd, p_ready)
            dve.wait_ge(vec_here, 16)
            dve.wait_ge(gates_done, 1)
            nc.vector.tensor_scalar(gamma16[:], vec_sb[:, V_GAMMA:V_GAMMA + N], SIM_SCALE, None,
                                    ALU.mult).then_inc(gamma_ready, 1)
            nc.vector.tensor_scalar(edge_c[:, 0:1], tg[:, 1:2], 0.3, None, ALU.mult).then_inc(edge_c_ready, 1)
            nc.vector.tensor_scalar(edge_c[:, 1:2], tg[:, 1:2], 0.4, None, ALU.mult)
            nc.vector.tensor_copy(val16[:].rearrange("p i q -> p (i q)"), cf[:, C_VAL:C_VAL + 4 * NT])

            def score_bank(i):
                return psum[SCORES[i % 4]][:, 0:N]

            def score_stats(b):
                dve.wait_ge(sim_done, 2 * b + 2)
                stats(score_bank, b, SIM_EPS, SIM_SCALE * SIM_SCALE, s_var)

            def norm_terms(b, rstd, signal):
                two = slice(2 * b, 2 * b + 2)
                dve.wait_ge(rstd, b + 1)
                nc.vector.scalar_tensor_tensor(out=off[:, two], in0=mv[:, two, 0], scalar=-1.0, in1=rs[:, two],
                                               op0=ALU.mult, op1=ALU.mult).then_inc(signal, 1)

            def score_shift(b):
                for i in (2 * b, 2 * b + 1):
                    dve.wait_ge(z_scaled, i + 1)
                    last = did(nc.vector.tensor_tensor_reduce(
                        out=z[:, i % 4, :], in0=z[:, i % 4, :], in1=vec_sb[:, V_BETA:V_BETA + N], scale=1.0,
                        scalar=NEVER, op0=ALU.add, op1=ALU.max, accum_out=mx[:, i:i + 1]))
                after(last)
                nc.vector.tensor_scalar(nmx[:, 2 * b:2 * b + 2], mx[:, 2 * b:2 * b + 2], -1.0, None,
                                        ALU.mult).then_inc(z_ready, 1)

            def attend(b):
                dve.wait_ge(exp_done, 2 * b + 2)
                then(nc.vector.reciprocal(rc[:, 2 * b:2 * b + 2], sm[:, 2 * b:2 * b + 2]))
                then(nc.vector.tensor_scalar(cc[:, 2 * b:2 * b + 2], rc[:, 2 * b:2 * b + 2], tg[:, 0:1], None,
                                             ALU.mult))
                for i in (2 * b, 2 * b + 1):
                    last = did(nc.vector.scalar_tensor_tensor(
                        out=xs[:, i, :], in0=e[:, i % 2, :], scalar=cc[:, i:i + 1], in1=xs[:, i, :],
                        op0=ALU.mult, op1=ALU.add))
                after(last)
                stats(rows_of_x, b, LN_EPS, 1.0, mix[0].var)

            score_stats(0)
            for b in range(B):
                norm_terms(b, s_rstd, s_terms)
                if b >= 1:
                    attend(b - 1)
                if b + 1 < B:
                    score_stats(b + 1)
                score_shift(b)
                if b >= 1:
                    norm_terms(b - 1, mix[0].rstd, mix[0].terms)
            attend(B - 1)
            norm_terms(B - 1, mix[0].rstd, mix[0].terms)

            def route(m):
                E = m.E
                desc = cf[:, C_DESC:C_DESC + E]
                lt = cf[:, C_LT:C_LT + E1 * E1].rearrange("p (a b) -> p a b", a=E1)[:, 0:E, 0:E]

                def wide(v):
                    return v.unsqueeze(2).to_broadcast([P, v.shape[1], E])

                def first_best(i, logits, best, onehot):
                    then(nc.vector.tensor_reduce(out=best, in_=logits, axis=X, op=ALU.max))
                    if i.stop - i.start == 2:
                        for n, j in enumerate(range(i.start, i.stop)):
                            last = did(nc.vector.scalar_tensor_tensor(
                                out=m.w[:, j], in0=logits[:, n], scalar=best[:, n:n + 1], in1=desc,
                                op0=ALU.is_equal, op1=ALU.mult))
                        after(last)
                    else:
                        then(nc.vector.tensor_tensor(m.w[:, i], logits, wide(best), ALU.is_equal))
                        then(nc.vector.tensor_tensor(m.w[:, i], m.w[:, i], desc.unsqueeze(1).to_broadcast(
                            [P, i.stop - i.start, E]), ALU.mult))
                    then(nc.vector.tensor_reduce(out=m.m[:, i], in_=m.w[:, i], axis=X, op=ALU.max))
                    then(nc.vector.tensor_tensor(onehot, m.w[:, i], wide(m.m[:, i]), ALU.is_equal))

                nc.vector.memset(m.A[:, NT, :], 0.0)
                parts = (slice(0, NT - 2), slice(NT - 2, NT))
                for i, logits in zip(parts, m.logits):
                    dve.wait_ge(m.logits_done, i.stop)
                    first_best(i, logits, m.v1[:, i], m.oh[:, 0, i])
                    then(nc.vector.scalar_tensor_tensor(out=m.L2[:, i], in0=m.oh[:, 0, i], scalar=NEVER,
                                                        in1=logits, op0=ALU.mult, op1=ALU.add))
                    first_best(i, m.L2[:, i], m.v2[:, i], m.oh[:, 1, i])
                    last = nc.vector.tensor_tensor(m.A[:, i, :], m.oh[:, 0, i], m.oh[:, 1, i], ALU.add)
                last.then_inc(m.picked, 1)
                if m.n == 1:
                    for i, logits in zip(parts, m.logits):
                        nc.vector.tensor_tensor(m.L2[:, i], logits, wide(m.v1[:, i]), ALU.subtract)
                nc.vector.tensor_tensor(m.d, m.v2, m.v1, ALU.subtract).then_inc(m.shifted, 1)

                dve.wait_ge(m.ranks_done, 1)
                then(nc.vector.tensor_tensor(
                    m.cmp, m.ranks[:, NT, :].unsqueeze(2).to_broadcast([P, E, NT]),
                    cf[:, C_THR:C_THR + NT].unsqueeze(1).to_broadcast([P, E, NT]), ALU.is_gt))
                then(nc.vector.tensor_reduce(out=m.tl, in_=m.cmp, axis=X, op=ALU.add))
                then(nc.vector.tensor_tensor(m.lt, lt, m.tl.unsqueeze(1).to_broadcast([P, E, E]), ALU.mult))
                then(nc.vector.tensor_reduce(out=m.base, in_=m.lt, axis=X, op=ALU.add))
                then(nc.vector.scalar_tensor_tensor(
                    out=m.R2, in0=m.base.unsqueeze(1).to_broadcast([P, NT, E]), scalar=float(P),
                    in1=m.ranks[:, 0:NT, :], op0=ALU.mult, op1=ALU.add))
                then(nc.vector.tensor_tensor(m.w12, m.oh,
                                             m.R2.unsqueeze(1).to_broadcast([P, 2, NT, E]), ALU.mult))
                then(nc.vector.tensor_reduce(out=m.lof, in_=m.w12.rearrange("p k i e -> p (k i) e"),
                                             axis=X, op=ALU.add))
                then(nc.vector.tensor_copy(m.place, m.lof))
                nc.vector.tensor_scalar(m.lo, m.place, P - 1, None, ALU.bitwise_and)
                then(nc.vector.tensor_scalar(m.hi, m.place, 7, None, ALU.logical_shift_right))
                nc.vector.tensor_copy(m.lof, m.lo)
                then(nc.vector.tensor_tensor(
                    hi1[:, :, 0:m.S], cf[:, C_SLOT:C_SLOT + m.S].unsqueeze(1).to_broadcast([P, 2 * NT, m.S]),
                    m.hi.unsqueeze(2).to_broadcast([P, 2 * NT, m.S]), ALU.is_equal))
                for q in range(2):
                    nc.vector.tensor_tensor(
                        hi2[:, :, q, 0:m.S], hi1[:, :, 0:m.S],
                        val16[:, :, q:q + 1].to_broadcast([P, 2 * NT, m.S]), ALU.mult)
                for i in range(2 * NT):
                    nc.vector.tensor_scalar(lo1[:, i, :], ch[:, H_LO:H_LO + P], m.lof[:, i:i + 1], None,
                                            ALU.is_equal).then_inc(m.onehots_ready, 1)
                dve.wait_ge(m.inverse_done, 1)
                nc.vector.tensor_copy(m.tok, m.inverse[:, 0, :]).then_inc(m.tokens_ready, 1)
                then(nc.vector.tensor_tensor(m.incl, m.base, m.tl, ALU.add))
                then(nc.vector.tensor_tensor(
                    m.scmp[0:1], cf[0:1, C_SLOT:C_SLOT + m.S].unsqueeze(2).to_broadcast([1, m.S, E - 1]),
                    m.incl[0:1, 0:E - 1].unsqueeze(1).to_broadcast([1, m.S, E - 1]), ALU.is_ge))
                then(nc.vector.tensor_reduce(out=m.ownf[0:1, :], in_=m.scmp[0:1], axis=X, op=ALU.add))
                nc.vector.tensor_copy(m.owner[0:1, :], m.ownf[0:1, :]).then_inc(m.experts_ready, 1)
                then(nc.vector.scalar_tensor_tensor(out=m.pad, in0=m.inverse[:, 1, :], scalar=0.0,
                                                    in1=cf[:, C_PAD:C_PAD + m.S], op0=ALU.is_equal, op1=ALU.mult))
                nc.vector.scalar_tensor_tensor(out=m.dst, in0=m.inverse[:, 1, :], scalar=-1.0, in1=m.pad,
                                               op0=ALU.add, op1=ALU.add).then_inc(m.targets_ready, 1)
                dve.wait_ge(m.exps, m.n + 1)
                if m.n == 0:
                    then(nc.vector.tensor_scalar(m.den, m.ed, 1.0, None, ALU.add))
                else:
                    then(nc.vector.tensor_reduce(out=m.den, in_=m.L2, axis=X, op=ALU.add))
                then(nc.vector.reciprocal(m.p1, m.den))
                then(nc.vector.tensor_scalar(m.c1, m.p1, tg[:, 2 + m.n:3 + m.n], None, ALU.mult))
                then(nc.vector.tensor_tensor(m.c2, m.c1, m.ed, ALU.mult))

            route(mix[0])

            def copy_hT(m, s, r):
                dve.wait_ge(m.hT_done, s + 1)
                if m.n == 0:
                    nc.vector.tensor_scalar(hT[:, 512:640], psum[5][:, 0:P], 0.5, None, ALU.mult)
                    nc.vector.tensor_scalar(hT[0:KF0[-1][1], 640:768], psum[5][0:KF0[-1][1], P:2 * P], 0.5, None,
                                            ALU.mult).then_inc(m.hT_copied_v, 1)
                else:
                    nc.vector.tensor_scalar(hT[0:KF1[-1][1], P:2 * P], psum[5][0:KF1[-1][1], 0:P], 0.5, None,
                                            ALU.mult).then_inc(m.hT_copied_v, 1)

            def hidden(m, t, r, half_step, halves=(0, 1)):
                if m.n == 0:
                    for c in halves:
                        cols = slice(c * CH0, (c + 1) * CH0)
                        dve.wait_ge(m.th_done, 2 * t + c + 1)
                        nc.vector.scalar_tensor_tensor(out=hh[:, cols], in0=th[:, cols], scalar=1.0,
                                                       in1=psum[2 * c][:, 0:CH0], op0=ALU.add,
                                                       op1=ALU.mult).then_inc(half_step, 1)
                        dve.wait_ge(half_step, 2 * t + c + 1)
                        nc.vector.tensor_tensor(hh[:, cols], hh[:, cols], psum[2 * c + 1][:, 0:CH0],
                                                ALU.mult).then_inc(m.h_made, 1)
                else:
                    cols = slice(r * F1, (r + 1) * F1)
                    dve.wait_ge(m.th_done, t + 1)
                    since(dve, m.hT_done, t - 1)
                    nc.vector.scalar_tensor_tensor(out=hh[:, cols], in0=th[:, cols], scalar=1.0,
                                                   in1=psum[r][:, 0:F1], op0=ALU.add,
                                                   op1=ALU.mult).then_inc(half_step, 1)
                    dve.wait_ge(half_step, t + (1 - NT))
                    nc.vector.tensor_tensor(hh[:, cols], hh[:, cols], psum[r][:, F1:2 * F1],
                                            ALU.mult).then_inc(m.h_made, 1)

            def copy_xT(m, t, r):
                dve.wait_ge(m.xT_done, t + 1)
                nc.vector.tensor_copy(xT[:, r, :], psum[6][:, 0:H]).then_inc(m.xT_copied, 1)

            m = mix[0]
            copy_xT(m, 0, 0)
            hidden(m, 0, 0, m.half)
            copy_xT(m, 1, 1)

            def step0(s, r):
                copy_hT(m, s, r)
                if below(s, m.S - 1):
                    hidden(m, s + 1, r, m.half, (0,))
                if below(s, m.S - 2):
                    copy_xT(m, s + 2, r % 2)
                if below(s, m.S - 1):
                    hidden(m, s + 1, r, m.half, (1,))

            steps(dve, step0, m.S, m.S - 2)

            def combine(m, b):
                dve.wait_ge(m.y_here[b], 16)
                ends = [did(nc.vector.scalar_tensor_tensor(
                    out=xs[:, i, :], in0=y_got[:, i, 0, :], scalar=m.c1[:, i:i + 1], in1=xs[:, i, :],
                    op0=ALU.mult, op1=ALU.add)) for i in (2 * b, 2 * b + 1)]
                for i, end in zip((2 * b, 2 * b + 1), ends):
                    after(end)
                    nc.vector.scalar_tensor_tensor(
                        out=xs[:, i, :], in0=y_got[:, i, 1, :], scalar=m.c2[:, i:i + 1], in1=xs[:, i, :],
                        op0=ALU.mult, op1=ALU.add).then_inc(m.x_new, 1)

            m1 = mix[1]

            def second(b):
                if b == 0:
                    combine(mix[0], b)
                else:
                    for i in (2 * b, 2 * b + 1):
                        dve.wait_ge(first_added, i - 1)
                        nc.vector.scalar_tensor_tensor(
                            out=xs[:, i, :], in0=y_got[:, i, 1, :], scalar=mix[0].c2[:, i:i + 1], in1=xs[:, i, :],
                            op0=ALU.mult, op1=ALU.add).then_inc(mix[0].x_new, 1)
                dve.wait_ge(mix[0].x_new, 2 * b + 2)
                stats(rows_of_x, b, LN_EPS, 1.0, x2_var)

            def mix_terms(b):
                two = slice(2 * b, 2 * b + 2)
                dve.wait_ge(x2_rstd, b + 1)
                then(nc.vector.tensor_scalar(rc[:, two], rs[:, two], edge_c[:, 1:2], None, ALU.mult))
                nc.vector.tensor_scalar(cc[:, two], rc[:, two], 1.0, None, ALU.add)
                nc.vector.scalar_tensor_tensor(out=nmx[:, two], in0=mv[:, two, 0], scalar=-1.0, in1=rc[:, two],
                                               op0=ALU.mult, op1=ALU.mult).then_inc(mix_ready, 1)

            def add_edge(b):
                for i in (2 * b, 2 * b + 1):
                    dve.wait_ge(mixed, i + 1)
                    last = did(nc.vector.tensor_tensor(xs[:, i, :], edge[:, i, :], xn[:, i, :], ALU.add))
                after(last)
                stats(rows_of_x, b, LN_EPS, 1.0, m1.var)

            dve.wait_ge(edge_ready, NT)
            second(0)
            second(1)
            mix_terms(0)
            for b in range(B):
                if b + 2 < B:
                    second(b + 2)
                if b + 1 < B:
                    mix_terms(b + 1)
                add_edge(b)
                if b >= 1:
                    norm_terms(b - 1, m1.rstd, m1.terms)
            norm_terms(B - 1, m1.rstd, m1.terms)
            route(m1)

            copy_xT(m1, 0, 0)
            copy_xT(m1, 1, 1)
            dve.wait_ge(m1.h_made, NT)
            hidden(m1, NT, 0, m1.half)
            copy_xT(m1, 2, 0)
            hidden(m1, NT + 1, 1, m1.half)

            def step1(s, r):
                copy_hT(m1, s + NT, r)
                if below(s, m1.S - 3):
                    copy_xT(m1, s + 3, (r + 1) % 2)
                if below(s, m1.S - 2):
                    hidden(m1, s + (NT + 2), r % 2, m1.half)

            steps(dve, step1, m1.S, m1.S - 3)
            dve.wait_ge(z_added, NT)
            for b in range(B):
                combine(m1, b)

        @block.tensor
        def _(pe):
            mm = nc.tensor.matmul

            def turn(dst, src):
                return nc.tensor.transpose(dst, src, cf[:, C_ID:C_ID + P])

            pe.wait_ge(small_here, 16)
            ctx_all = small_sb[0:D + 1, M_CTX:M_CTX + T]
            wk = small_sb[0:D + 1, M_WK:M_WK + D]
            for i in range(NT):
                last = mm(psum[5][:, i * D:(i + 1) * D], ctx_all[:, i * P:(i + 1) * P], wk, start=True, stop=True)
            last.then_inc(kv_done, 1)
            pe.wait_ge(const_here, 16)

            def keys(h):
                mm(psum[3 + 3 * h][0:D, :], wk, ctx_all[:, h * 512:(h + 1) * 512], start=True,
                   stop=True).then_inc(kvT_done, 1)

            def turn_p(i):
                pe.wait_ge(p_ready, i + 1)
                since(pe, pT_copied, i - 1)
                for k in range(KH):
                    last = turn(psum[i % 2][:, k * P:(k + 1) * P], xn[:, i, k * P:(k + 1) * P])
                last.then_inc(pT_done, 1)

            def attend(i):
                if i == 0:
                    pe.wait_ge(kv_copied, 1)
                pe.wait_ge(pT_copied, i + 1)
                since(pe, oT_copied, i)
                for k in range(KH):
                    last = mm(psum[2][0:D, 0:P], kv[:, 2 * (i // 2) + k, :], pT[:, i % 2, k * P:(k + 1) * P],
                              start=(k == 0), stop=(k == KH - 1))
                last.then_inc(oT_done, 1)

            def score(i):
                pe.wait_ge(kvT_copied, 1 + i // 4)
                pe.wait_ge(oT_copied, i + 1)
                since(pe, s_read, i - 3)
                b = i // 2
                mm(psum[SCORES[i % 4]][:, 0:N], oT[:, i, :], kvT[:, b * N:(b + 1) * N], start=True,
                   stop=True).then_inc(sim_done, 1)

            def turn_xn(m, i):
                pe.wait_ge(m.xn_ready, i + 1)
                since(pe, m.xnT_copied, i - 1)
                for k in range(KH):
                    last = turn(psum[i % 2][:, k * P:(k + 1) * P], xn[:, i, k * P:(k + 1) * P])
                last.then_inc(m.xnT_done, 1)

            def logits(m, i, src):
                pe.wait_ge(m.xnT_copied, i + 1)
                rw = router_sb[:, :, 0:E0] if m.n == 0 else router_sb[:, :, E0:E0 + E1]
                for k in range(KH):
                    last = mm(m.logits[i // (NT - 2)][:, i % (NT - 2), :], src[:, k * P:(k + 1) * P], rw[:, k, :],
                              start=(k == 0), stop=(k == KH - 1))
                last.then_inc(m.logits_done, 1)

            def ranks(m):
                pe.wait_ge(m.picked, 1)
                mm(m.ranks, ch[:, H_TRI:H_TRI + P], m.A, start=True, stop=False)
                for i in range(NT):
                    last = mm(m.ranks[:, i + 1:NT + 1, :], ch[:, H_ONE:H_ONE + P],
                              m.A[:, i:i + 1, :].to_broadcast([P, NT - i, m.E]), start=False, stop=(i == NT - 1))
                last.then_inc(m.ranks_done, 1)

            def inverse(m):
                for i in range(2 * NT):
                    pe.wait_ge(m.onehots_ready, i + 1)
                    last = mm(m.inverse, lo1[:, i, :], hi2[:, i, :, 0:m.S], start=(i == 0), stop=(i == 2 * NT - 1))
                last.then_inc(m.inverse_done, 1)

            turn_p(0)
            turn_p(1)
            keys(0)
            attend(0)
            turn_p(2)
            attend(1)
            score(0)
            turn_p(3)
            score(1)
            attend(2)
            keys(1)
            wj = small_sb[0:D + 1, M_WJ:M_WJ + P]
            wi = small_sb[0:D + 1, M_WI:M_WI + 1]

            def edges(h):
                mm(psum[6 - 5 * h][:, :], wj, ctx_all[:, h * 512:(h + 1) * 512], start=True,
                   stop=True).then_inc(sj_done, 1)

            for i in range(3, NT):
                if i + 1 < NT:
                    turn_p(i + 1)
                attend(i)
                if i <= 4:
                    score(i - 1)
                if i == 4:
                    pe.wait_ge(kvT_copied, 2)
                    edges(0)
            score(4)
            score(5)
            pe.wait_ge(oT_copied, NT)
            for i in range(NT):
                last = mm(psum[2][:, i:i + 1], ctx_all[:, i * P:(i + 1) * P], wi, start=True, stop=True)
            last.then_inc(si_done, 1)
            pe.wait_ge(pT_copied, NT)
            edges(1)
            score(6)
            score(7)
            pe.wait_ge(router_here, 16)
            turn_xn(mix[0], 0)
            pe.wait_ge(edge_th, NT)
            for i in range(NT):
                if i + 1 < NT:
                    turn_xn(mix[0], i + 1)
                logits(mix[0], i, xT[:, i % 2, :])
            pe.wait_ge(constb_here, 16)
            ranks(mix[0])
            inverse(mix[0])

            def turn_x(m, t, r):
                pe.wait_ge(m.x_loaded[r], landed(t, r))
                since(pe, m.xT_copied, t)
                for k in range(KH):
                    last = turn(psum[6][:, k * P:(k + 1) * P], x_in[:, r, k * P:(k + 1) * P])
                last.then_inc(m.xT_done, 1)

            def turn_h(m, s, r):
                base = 0 if m.n == 0 else r * F1
                pe.wait_ge(m.h_made, (s + 1) * (2 if m.n == 0 else 1))
                for j, n in m.kf:
                    bank, col = (4, j * P) if j < m.split else (5, (j - m.split) * P)
                    last = nc.tensor.transpose(psum[bank][0:n, col:col + P],
                                               hh[:, base + j * P:base + j * P + n], cf[:, C_ID:C_ID + P])
                last.then_inc(m.hT_done, 1)

            def down(m, s, wd):
                pe.wait_ge(m.hT_copied_a, s + 1)
                pe.wait_ge(m.hT_copied_v, s + 1)
                for j, n in m.kf:
                    last = mm(psum[7][:, 0:H], hT[0:n, j * P:(j + 1) * P], wd(j, n),
                              start=(j == 0), stop=(j == len(m.kf) - 1))
                last.then_inc(m.y_done, 1)

            m = mix[0]

            def owner(m, t):
                return pe.value_load(m.owner[0:1, bass.ds(t, 1)], min_val=0, max_val=m.E - 1)

            def gate_up0(t, r):
                at = owner(m, t) * GU0
                pe.wait_ge(m.xT_copied, t + 1)
                for c in range(2):
                    for g in range(2):
                        for k in range(KH):
                            last = mm(psum[2 * c + g][:, 0:CH0], xT[:, r, k * P:(k + 1) * P],
                                      wgu[:, bass.ds(at + (k * 4 + 2 * c + g) * CH0, CH0)],
                                      start=(k == 0), stop=(k == KH - 1))
                    last.then_inc(m.gu_done, 1)

            def down0(s, r):
                at = owner(m, s) * WD0
                since(pe, m.y_copied, s)
                down(m, s, lambda j, n: wdn[0:n, bass.ds(at + j * H, H)])

            pe.wait_ge(m.experts_ready, 1)
            turn_x(m, 0, 0)
            pe.wait_ge(w0_here[0], 48)
            gate_up0(0, 0)
            turn_x(m, 1, 1)

            def step0(s, r):
                turn_h(m, s, r)
                if isinstance(s, int) and s < RING:
                    for n in ([s + 1] if s < RING - 1 else range(RING, E0)):
                        pe.wait_ge(w0_here[n], 48)
                if below(s, m.S - 1):
                    gate_up0(s + 1, (r + 1) % 2)
                if below(s, m.S - 2):
                    turn_x(m, s + 2, (r + 2) % RING)
                down0(s, r)

            steps(pe, step0, m.S, m.S - 2)

            m1 = mix[1]

            def gate_up1(r, src, at):
                for k in range(KH):
                    last = mm(psum[r][:, 0:2 * F1], src[:, k * P:(k + 1) * P],
                              wgu[:, bass.ds(at + k * 2 * F1, 2 * F1)], start=(k == 0), stop=(k == KH - 1))
                last.then_inc(m1.gu_done, 1)

            def gate_up_slots(t, r, expert):
                at = expert * GU1 + GU1
                pe.wait_ge(m1.xT_copied, t + 1)
                gate_up1(r, xT[:, r, :], at)

            pe.wait_ge(mix[0].y_copied, S0)
            turn_xn(m1, 0)
            for i in range(NT):
                if i + 1 < NT:
                    turn_xn(m1, i + 1)
                logits(m1, i, xnT[:, i, :])
            for n, (_, gu_a, gu_z, dn_a, dn_z) in enumerate(second_weights()):
                pe.wait_ge(w1_here[n], 16 * (gu_z > gu_a) + 32 * (dn_z > dn_a))
            for i in range(2):
                gate_up1(i, xnT[:, i, :], SHARED)
            ranks(m1)
            for i in range(NT):
                if i == NT // 2:
                    inverse(m1)
                turn_h(m1, i, i % 2)
                if i + 2 < NT:
                    gate_up1(i % 2, xnT[:, i + 2, :], SHARED)
                if i == NT - 1:
                    turn_x(m1, 0, 0)
                    pe.wait_ge(m1.experts_ready, 1)
                    gate_up_slots(0, 0, owner(m1, 0))
                since(pe, z_copied, i)
                down(m1, i, lambda j, n: wdn[0:n, j * H:(j + 1) * H])
            turn_x(m1, 1, 1)
            gate_up_slots(1, 1, owner(m1, 1))
            turn_x(m1, 2, 2)

            def step1(s, r):
                turn_h(m1, s + NT, r % 2)
                if below(s, m1.S - 2):
                    gate_up_slots(s + 2, r % 2, owner(m1, s + 2))
                if below(s, m1.S - 3):
                    turn_x(m1, s + 3, (r + 3) % RING)
                if isinstance(s, int) and s == 0:
                    pe.wait_ge(z_copied, NT)
                at = owner(m1, s) * WD1 + WD1
                since(pe, m1.y_copied, s)
                down(m1, s + NT, lambda j, n: wdn[0:n, bass.ds(at + j * H, H)])

            steps(pe, step1, m1.S, m1.S - 3)


def _constants():
    import numpy as np
    c = np.zeros((P, C_ALL), np.float32)
    c[:, C_ID:C_ID + P] = np.eye(P)
    c[:, C_DESC:C_DESC + 16] = 16 - np.arange(16)
    c[:, C_THR:C_THR + NT] = [-1] + [P * i for i in range(1, NT)]
    c[:, C_LT:C_LT + E1 * E1] = np.tril(np.ones((E1, E1)), -1).ravel()
    c[:, C_SLOT:C_SLOT + S1] = np.arange(S1)
    c[:, C_NH] = -0.5
    token = P * np.arange(NT)[None, :, None] + np.arange(P)[:, None, None]
    token, pick = np.broadcast_arrays(token[:, None], np.arange(2)[None, :, None, None])
    c[:, C_VAL:C_VAL + 4 * NT] = np.concatenate([token, 2 * token + pick + 1], 3).reshape(P, 4 * NT)
    c[:, C_PAD:C_PAD + S1] = 2 * T + 1 + P * np.arange(S1)[None] + np.arange(P)[:, None]
    half = np.concatenate([np.triu(np.ones((P, P)), 1), np.ones((P, P)),
                           np.broadcast_to(np.arange(P), (P, P))], 1)
    return c, half.astype(np.float16)


def kernel(**inputs):
    import numpy as np
    import concourse.bacc as bacc
    from concourse.bass_utils import run_bass_kernel_spmd

    a = {k: np.asarray(v) for k, v in inputs.items()}
    f32 = np.float32
    const_f, const_h = _constants()

    small = np.zeros((M_ROWS, M_ALL), f32)
    small[0:D, M_CTX:M_CTX + T] = a["ctx_512"].reshape(T, D).T
    small[D, M_CTX:M_CTX + T] = 1.0
    small[0:D, M_WK:M_WK + D] = a["L0_xattn_W_k"].T
    small[D, M_WK:M_WK + D] = a["L0_xattn_b_k"]
    small[0:D, M_WJ:M_WJ + P] = a["L1_xattn_W"][0, D:, None]
    small[D, M_WJ:M_WJ + P] = a["L1_xattn_b"][0]
    small[0:D, M_WI] = a["L1_xattn_W"][0, :D]
    vecs = np.concatenate([a["L0_xattn_ln_gamma"], a["L0_xattn_ln_beta"], a["g_xattn"], a["g_ffn"]])[None]
    router = np.concatenate([a["L0_ffn_router_w"], a["L1_ffn_gate_w"]], 0).T.reshape(KH, P, E0 + E1)

    def split(w, halves):
        e, f, _ = w.shape
        return w.reshape(e, halves, f // halves, KH, P).transpose(0, 4, 3, 1, 2)

    def shared_first(w, s):
        return np.concatenate([s[None], w], 0)

    gu0 = np.stack([split(a["L0_ffn_gate_w"], 2), split(a["L0_ffn_up_w"], 2)], 4)
    gu1 = np.stack([split(shared_first(a["L1_ffn_w1"], a["L1_ffn_sw1"]), 1),
                    split(shared_first(a["L1_ffn_w3"], a["L1_ffn_sw3"]), 1)], 4)
    d0 = a["L0_ffn_down_w"].transpose(0, 2, 1)
    d1 = shared_first(a["L1_ffn_w2"], a["L1_ffn_sw2"]).transpose(0, 2, 1)
    cut = (len(KF0) - 1) * P
    arrays = {
        "x": a["x"].reshape(T, H), "small": small, "vecs": vecs, "router": router.transpose(1, 0, 2),
        "const_f": const_f, "const_h": const_h,
        "gu0": gu0.reshape(E0, P, GU0),
        "wd0a": d0[:, :cut].reshape(E0, cut // P, P, H).transpose(0, 2, 1, 3).reshape(E0, P, cut // P * H),
        "wd0b": d0[:, cut:],
        "gu1": gu1.reshape(E1 + 1, P, GU1), "wd1a": d1[:, :P], "wd1b": d1[:, P:],
    }
    arrays = {k: np.ascontiguousarray(v) for k, v in arrays.items()}
    nc = bacc.Bacc("TRN2", target_bir_lowering=False, num_devices=1)
    aps = [nc.dram_tensor(k, v.shape, mybir.dt.from_np(v.dtype), kind="ExternalInput").ap() for k, v in arrays.items()]
    out = nc.dram_tensor("out", (T, H), mybir.dt.float32, kind="ExternalOutput").ap()
    build(nc, *aps, out)
    r = run_bass_kernel_spmd(nc, [arrays], core_ids=[0])
    return r.results[0]["out"].reshape(B, N, H)
```
